# Optimizing a Trainium2 kernel written in Bass

```python
import numpy as np
import jax
import jax.numpy as jnp

def _softmax(x, axis=-1):
    return jax.nn.softmax(x, axis=axis)

def _gelu(x):
    return jax.nn.gelu(x, approximate=True)

def _silu(x):
    return jax.nn.silu(x)

def _sigmoid(x):
    return jax.nn.sigmoid(x)

def _layernorm(x, axis=-1, eps=1e-05):
    m = jnp.mean(x, axis=axis, keepdims=True)
    v = jnp.var(x, axis=axis, keepdims=True)
    return (x - m) / jnp.sqrt(v + eps)

def _scatter_add(tgt, idx, src, axis=0):
    return tgt.at[idx].add(src)

def _segment_sum(src, seg, n):
    return jax.ops.segment_sum(src, seg, n)
kernel_name = 'mk_decoder_postln_d1_seqx_r8_fc321d'

def setup_inputs(seed: int=0):
    np.random.seed(seed)
    _w = jnp.asarray

    def _rec_inputs():
        import jax
        import jax.numpy as jnp
        _rk = jax.random.key(seed)
        x = 7.22e-05 + 1 * jax.random.normal(jax.random.fold_in(_rk, 1), (8, 128, 512), jnp.float32)
        _lenS = 128 - jax.random.randint(jax.random.fold_in(_rk, 7), (8,), 0, max(1, 128 // 4) + 1, jnp.int32)
        _lenS2 = 128 - jax.random.randint(jax.random.fold_in(_rk, 8), (8,), 0, max(1, 128 // 4) + 1, jnp.int32)
        _ctx_4096P = jax.random.normal(jax.random.fold_in(_rk, 11), (8, 16, 512), jnp.float32)
        _ctx_4096c = jax.random.dirichlet(jax.random.fold_in(_rk, 511), 0.3 * jnp.ones((16,), jnp.float32), (8, 128))
        _ctx_4096t = jnp.einsum('bsk,bkd->bsd', _ctx_4096c, _ctx_4096P)
        _ctx_4096t = _ctx_4096t * jax.lax.rsqrt(jnp.mean(jnp.square(_ctx_4096t)) + 1e-12) * 0.953939
        ctx_4096 = 4.13588e-05 + 0.999923 * (_ctx_4096t + 0.3 * jax.random.normal(jax.random.fold_in(_rk, 611), (8, 128, 512), jnp.float32))
        _validS = jnp.arange(128)[None, :] < _lenS[:, None]
        _validS2 = jnp.arange(128)[None, :] < _lenS2[:, None]
        _causal = jnp.tril(jnp.ones((128, 128), dtype=bool))
        mask_BxSxS2_bk0 = jnp.logical_not(jnp.broadcast_to(_validS2[:, None, :], (8, 128, 128)))
        return (x, ctx_4096, mask_BxSxS2_bk0)
    x, ctx_4096, mask_BxSxS2_bk0 = _rec_inputs()

    def _L0_attn_setup():
        import jax, jax.numpy as jnp
        import numpy as np
        import math
        FACTOR = 1
        key = jax.random.key(seed)
        x = jax.random.normal(key, (8, 64, 512), dtype=jnp.float32)
        return {'x': x}
    _L0_attn_all = _L0_attn_setup()
    _L0_attn_in = {k: v for k, v in _L0_attn_all.items() if k in ()}
    del _L0_attn_all

    def _L0_xattn_setup():
        import jax, jax.numpy as jnp
        import numpy as np
        B, LQ, LK, D, H, DH = (2, 128, 128, 512, 32, 128)
        EPS = 1e-05

        def _rmsnorm(x, weight):
            var = jnp.mean(jnp.square(x), axis=-1, keepdims=True)
            return x * jax.lax.rsqrt(var + EPS) * weight
        key = jax.random.key(seed)
        ks = jax.random.split(key, 8)
        scale = 0.02
        return {'hidden_states': jax.random.normal(ks[0], (B, LQ, D), jnp.float32), 'key_value_states': jax.random.normal(ks[1], (B, LK, D), jnp.float32), 'attention_mask': jax.random.randint(ks[2], (B, LQ, LK), 0, 2) > 0, 'position_bias': jax.random.normal(ks[3], (H, LQ, LK), jnp.float32), 'ln_weight': jnp.ones((D,), jnp.float32), 'w_q': jax.random.normal(ks[4], (H * DH, D), jnp.float32) * scale, 'w_k': jax.random.normal(ks[5], (H * DH, D), jnp.float32) * scale, 'w_v': jax.random.normal(ks[6], (H * DH, D), jnp.float32) * scale, 'w_out': jax.random.normal(ks[7], (D, H * DH), jnp.float32) * scale}
    _L0_xattn_all = _L0_xattn_setup()
    _L0_xattn_in = {k: v for k, v in _L0_xattn_all.items() if k in ('position_bias', 'ln_weight', 'w_q', 'w_k', 'w_v', 'w_out')}
    del _L0_xattn_all

    def _L0_ffn_setup():
        import jax, jax.numpy as jnp
        import numpy as np
        HID, INT, LAT, NE, K = (512, 1024, 256, 8, 2)
        LN_EPS = 1e-05

        def _layernorm(x, gamma, beta):
            mu = jnp.mean(x, axis=-1, keepdims=True)
            var = jnp.var(x, axis=-1, keepdims=True)
            return (x - mu) * jax.lax.rsqrt(var + LN_EPS) * gamma + beta
        key = jax.random.key(seed)
        ks = jax.random.split(key, 8)
        s = lambda d: 1.0 / np.sqrt(d)
        return {'hidden_states': jax.random.normal(ks[0], (4, 256, HID), jnp.float32), 'gate_w': jax.random.normal(ks[1], (HID, NE), jnp.float32) * s(HID), 'up_w': jax.random.normal(ks[2], (HID, INT), jnp.float32) * s(HID), 'down_w': jax.random.normal(ks[3], (INT, HID), jnp.float32) * s(INT), 'fc1_w': jax.random.normal(ks[4], (HID, LAT), jnp.float32) * s(HID), 'fc2_w': jax.random.normal(ks[5], (LAT, HID), jnp.float32) * s(LAT), 'expert_w': jax.random.normal(ks[6], (LAT, LAT), jnp.float32), 'ln_gamma': jnp.ones((HID,), jnp.float32), 'ln_beta': jnp.zeros((HID,), jnp.float32)}
    _L0_ffn_all = _L0_ffn_setup()
    _L0_ffn_in = {k: v for k, v in _L0_ffn_all.items() if k in ('gate_w', 'up_w', 'down_w', 'fc1_w', 'fc2_w', 'expert_w', 'ln_gamma', 'ln_beta')}
    del _L0_ffn_all
    return {'x': x, 'ctx_4096': ctx_4096, 'mask_BxSxS2_bk0': mask_BxSxS2_bk0, 'L0_xattn_position_bias': _L0_xattn_in['position_bias'], 'L0_xattn_ln_weight': _L0_xattn_in['ln_weight'], 'L0_xattn_w_q': _L0_xattn_in['w_q'], 'L0_xattn_w_k': _L0_xattn_in['w_k'], 'L0_xattn_w_v': _L0_xattn_in['w_v'], 'L0_xattn_w_out': _L0_xattn_in['w_out'], 'L0_ffn_gate_w': _L0_ffn_in['gate_w'], 'L0_ffn_up_w': _L0_ffn_in['up_w'], 'L0_ffn_down_w': _L0_ffn_in['down_w'], 'L0_ffn_fc1_w': _L0_ffn_in['fc1_w'], 'L0_ffn_fc2_w': _L0_ffn_in['fc2_w'], 'L0_ffn_expert_w': _L0_ffn_in['expert_w'], 'L0_ffn_ln_gamma': _L0_ffn_in['ln_gamma'], 'L0_ffn_ln_beta': _L0_ffn_in['ln_beta']}

def reference(x, ctx_4096, mask_BxSxS2_bk0, L0_xattn_position_bias, L0_xattn_ln_weight, L0_xattn_w_q, L0_xattn_w_k, L0_xattn_w_v, L0_xattn_w_out, L0_ffn_gate_w, L0_ffn_up_w, L0_ffn_down_w, L0_ffn_fc1_w, L0_ffn_fc2_w, L0_ffn_expert_w, L0_ffn_ln_gamma, L0_ffn_ln_beta):
    import jax
    import jax.numpy as jnp

    def _L0_attn_ref(x):
        import jax, jax.numpy as jnp
        import numpy as np
        import math
        FACTOR = 1
        B, C, L = x.shape
        xh = x[:, None]
        f = jnp.fft.rfft(xh, axis=-1)
        corr = jnp.fft.irfft(f * jnp.conj(f), n=L, axis=-1)
        top_k = int(FACTOR * math.log(L))
        weights, delay = jax.lax.top_k(corr, top_k)
        tmp_corr = jax.nn.softmax(weights, axis=-1)
        init_index = jnp.arange(L)
        idx = (init_index[None, None, None, None, :] + delay[..., None]) % L
        pattern = jnp.take_along_axis(xh[:, :, :, None, :], idx, axis=-1)
        delays_agg = jnp.sum(pattern * tmp_corr[..., None], axis=-2)
        return delays_agg[:, 0]

    def _L0_xattn_ref(hidden_states, key_value_states, attention_mask, position_bias, ln_weight, w_q, w_k, w_v, w_out):
        import jax, jax.numpy as jnp
        import numpy as np
        B, LQ, LK, D, H, DH = (2, 128, 128, 512, 32, 128)
        EPS = 1e-05

        def _rmsnorm(x, weight):
            var = jnp.mean(jnp.square(x), axis=-1, keepdims=True)
            return x * jax.lax.rsqrt(var + EPS) * weight
        x = _rmsnorm(hidden_states, ln_weight)
        b, lq, _ = x.shape
        lk = key_value_states.shape[1]
        h_q = (x @ w_q.T).reshape(b, lq, H, DH)
        h_k = (key_value_states @ w_k.T).reshape(b, lk, H, DH)
        h_v = (key_value_states @ w_v.T).reshape(b, lk, H, DH)
        score = jnp.einsum('bqhd,bkhd->bhqk', h_q, h_k)
        score = score + position_bias[None]
        m = attention_mask[:, None]
        score = jnp.where(m, score, -jnp.inf)
        score = jax.nn.softmax(score, axis=-1)
        score = jnp.where(m, score, 0.0)
        attn = jnp.einsum('bhqk,bkhd->bqhd', score, h_v).reshape(b, lq, H * DH)
        out = attn @ w_out.T
        return hidden_states + out

    def _L0_ffn_ref(hidden_states, gate_w, up_w, down_w, fc1_w, fc2_w, expert_w, ln_gamma, ln_beta):
        import jax, jax.numpy as jnp
        import numpy as np
        HID, INT, LAT, NE, K = (512, 1024, 256, 8, 2)
        LN_EPS = 1e-05

        def _layernorm(x, gamma, beta):
            mu = jnp.mean(x, axis=-1, keepdims=True)
            var = jnp.var(x, axis=-1, keepdims=True)
            return (x - mu) * jax.lax.rsqrt(var + LN_EPS) * gamma + beta
        logits = jnp.einsum('bsh,he->bse', hidden_states, gate_w)
        routing_weights, selected_experts = jax.lax.top_k(logits, K)
        h = jax.nn.relu(jnp.einsum('bsh,hi->bsi', hidden_states, up_w)) ** 2
        shared_out = jnp.einsum('bsi,ih->bsh', h, down_w)
        x_latent = jnp.einsum('bsh,hl->bsl', hidden_states, fc1_w)
        expert_out = jnp.einsum('bsl,lm->bsm', x_latent, expert_w)
        moe_out = expert_out * jnp.sum(routing_weights, axis=-1, keepdims=True)
        routed_out = jnp.einsum('bsl,lh->bsh', moe_out, fc2_w)
        return _layernorm(shared_out + routed_out, ln_gamma, ln_beta)
    x = _layernorm(x + _L0_attn_ref(x), axis=-1)
    x = _layernorm(x + _L0_xattn_ref(x, ctx_4096, mask_BxSxS2_bk0, L0_xattn_position_bias, L0_xattn_ln_weight, L0_xattn_w_q, L0_xattn_w_k, L0_xattn_w_v, L0_xattn_w_out), axis=-1)
    x = _layernorm(x + _L0_ffn_ref(x, L0_ffn_gate_w, L0_ffn_up_w, L0_ffn_down_w, L0_ffn_fc1_w, L0_ffn_fc2_w, L0_ffn_expert_w, L0_ffn_ln_gamma, L0_ffn_ln_beta), axis=-1)
    return x

_drawn_inputs = setup_inputs


def setup_inputs(seed=0):
    import zlib

    import numpy as np

    out = dict(_drawn_inputs(seed))
    spreads = {'L0_xattn_ln_weight': (1.0, 0.2),
     'L0_ffn_ln_gamma': (1.0, 0.2),
     'L0_ffn_ln_beta': (0.0, 0.1)}
    factors = {}
    for name, (base, spread) in spreads.items():
        noise = np.random.default_rng([zlib.crc32(name.encode()), seed]).standard_normal(out[name].shape)
        drawn = base * np.exp(spread * noise) if base else spread * noise
        out[name] = jnp.asarray(drawn.astype(out[name].dtype))
    for name, factor in factors.items():
        out[name] = (out[name] * factor).astype(out[name].dtype)
    return out
```

```python
from contextlib import ExitStack

import concourse.bass as bass
from concourse import mybir
import numpy as np

F32 = mybir.dt.float32
F32R = mybir.dt.float32r
U32 = mybir.dt.uint32
U8 = mybir.dt.uint8
ALU = mybir.AluOpType
ACT = mybir.ActivationFunctionType
AX = mybir.AxisListType

P = 128
B = 8
D = 512
DC = D // P
TOK = B * P
HALF = TOK // 2
HB = B // 2
H = 32
PAIRS = H // 2
INT = 1024
IC = INT // P
LAT = 256
LC = LAT // P
NE = 8
LAGS = 6
EPS = 1e-5
FAR = 2.0 ** 100
PIECE = 1024
SLOTS = 4
RING = 4

DFT_PIECES = 7
LAST_LAG = D // 2
CTX_PIECES = DC
FFN_PIECES = 11

PC_WV0, PC_QK00, PC_QK01 = CTX_PIECES, CTX_PIECES + 1, CTX_PIECES + 2
LOOP0 = CTX_PIECES + 3


def build(nc, t):
    units = 4 * PAIRS
    with ExitStack() as ctx:
        def sb(name, shape, dt=F32):
            return ctx.enter_context(nc.sbuf_tensor(name, shape, dt))

        def sem(name):
            return ctx.enter_context(nc.semaphore(name))

        def hilo(name, shape):
            return sb(name + "_hi", shape, F32R), sb(name + "_lo", shape, F32R)

        xn = hilo("xn", [P, DC, TOK])
        cx = hilo("cx", [P, DC, TOK])
        acc = sb("acc", [P, B, D])
        wqk = hilo("wqk", [P, 2, 2, DC, P])
        wv = hilo("wv", [P, DC, 2 * P])
        wo = hilo("wo", [P, 2, D])
        vv = hilo("vv", [P, B, 2 * P])
        at = hilo("at", [P, 2, 2, HALF])
        qk_parts = sb("qk", [P, 2, 2, HALF], F32R)
        pt_parts = sb("pt", [P, 2, HB, P], F32R)
        qk = [qk_parts[:, i] for i in (0, 1)]
        pt = [pt_parts[:, i] for i in (0, 1)]
        rest = sb("rest", [P, HB, P])
        ext = hilo("ext", [P, 2, D])
        smx = sb("smx", [P, 4, HB, P])
        raw = sb("raw", [P, SLOTS, PIECE])
        far = sb("far", [P, B, P])
        bias = sb("bias", [P, 2, P])
        ident = sb("ident", [P, P])
        rows = sb("rows", [P, 2, D])
        lnw = sb("lnw", [P, D])
        m8 = sb("m8", [P, B, P], U8)
        scores_sb, exps, probs, bm = (smx[:, i] for i in range(4))

        gate = hilo("gate", [P, DC, NE])
        lg8 = sb("lg8", [P, B, 8])
        rsum = sb("rsum", [P, B, 1])
        half_pow = sb("half_pow", [P, 1])
        rowbase = sb("rowbase", [P, 1])
        topv = sb("topv", [P, B, 16])
        topi = sb("topi", [P, B, 8], U32)
        gidx = sb("gidx", [P, B, 8], U32)
        topm = sb("topm", [P, B, 3])
        ones = sb("ones", [P, 1])
        others = sb("others", [P, 2])
        nonzero = sb("nonzero", [P, 2])
        general = sb("general", [P, 2], mybir.dt.int32)
        wts = sb("wts", [P, B, 8])
        wsum = sb("wsum", [P, B, 2])
        st6 = sb("st6", [P, B, 6])
        mv = sb("mv", [P, B, 2])
        stat = sb("stat", [P, B, 6])
        prep = sb("prep", [P, 5, B])
        nmax = sb("nmax", [P, 2, HB])
        esum = sb("esum", [P, 3, HB])

        psum = ctx.enter_context(nc.psum_tensor("psum", [P, 8, 512], F32))
        banks = [psum[:, i] for i in range(8)]
        psQ, psK, psT, psV = banks[0:4]
        psO = [psK, psV]

        def parts(first):
            return psum[:, first:first + 2].rearrange("p k (b i n) -> p (k b) i n", b=2, i=2)

        psA, psS = parts(4), parts(6)

        s_dft_hi = sem("dft_hi")
        s_dft_lo = sem("dft_lo")
        s_w_hi = sem("w_hi")
        s_w_lo = sem("w_lo")
        s_consts = sem("consts")
        s_x_landed = sem("x_landed")
        s_mask_landed = sem("mask_landed")
        s_lnw_landed = sem("lnw_landed")
        s_far_ready = sem("far_ready")
        s_dft_mm = sem("dft_mm")
        s_sq_done = sem("sq_done")
        s_sq_hi = sem("sq_hi")
        s_sq_lo = sem("sq_lo")
        s_corr_mm = sem("corr_mm")
        s_top_val = sem("top_val")
        s_top_idx = sem("top_idx")
        s_gather_idx = sem("gather_idx")
        s_top_max = sem("top_max")
        s_w_exp = sem("w_exp")
        s_w_rec = sem("w_rec")
        s_w_ready = sem("w_ready")
        s_w0_ready = sem("w0_ready")
        s_acc_scaled = sem("acc_scaled")
        s_acc_sum = [sem(f"acc_sum{i}") for i in range(2)]
        s_stats_a = sem("stats_a")
        s_stats_b = sem("stats_b")
        s_var_eps = sem("var_eps")
        s_rstd = sem("rstd")
        s_x1_ready = sem("x1_ready")
        s_first_lo = sem("first_lo")
        s_mirrored = sem("mirrored")
        s_lag0 = sem("lag0")
        s_others = sem("others")
        s_nonzero = sem("nonzero")
        s_count_mm = sem("count_mm")
        s_general = sem("general")
        s_prep = sem("prep")
        s_rms = sem("rms")
        s_xn_ready = sem("xn_ready")
        s_acc_x1 = sem("acc_x1")
        s_xt_mm = sem("xt_mm")
        s_xt_hi = sem("xt_hi")
        s_xt_lo = sem("xt_lo")
        s_q_mm = sem("q_mm")
        s_q_hi = sem("q_hi")
        s_q_lo = sem("q_lo")
        s_k_mm = sem("k_mm")
        s_k_hi = sem("k_hi")
        s_k_lo = sem("k_lo")
        s_t_mm = sem("t_mm")
        s_t_hi = sem("t_hi")
        s_t_lo = sem("t_lo")
        s_v_mm = sem("v_mm")
        s_v_hi = sem("v_hi")
        s_v_lo = sem("v_lo")
        s_a_mm = sem("a_mm")
        s_a_hi = sem("a_hi")
        s_a_rest = sem("a_rest")
        s_a_lo = sem("a_lo")
        s_scores_mm = sem("scores_mm")
        s_scores_sum = sem("scores_sum")
        s_scores_full = sem("scores_full")
        s_scores_max = sem("scores_max")
        s_max_neg = sem("max_neg")
        s_exp_done = sem("exp_done")
        s_sum_clamped = sem("sum_clamped")
        s_sum_inverse = sem("sum_inverse")
        s_probs_ready = sem("probs_ready")
        s_bm_ready = sem("bm_ready")
        s_o_mm = sem("o_mm")
        s_o_add = sem("o_add")
        s_stored = sem("stored")
        s_f_lo = sem("f_lo")
        s_gate_hi = sem("gate_hi")
        s_gate_lo = sem("gate_lo")
        s_rows_landed = sem("rows_landed")
        s_y_stats_a = sem("y_stats_a")
        s_y_stats_b = sem("y_stats_b")
        s_y_eps = sem("y_eps")
        s_y_rstd = sem("y_rstd")
        s_x2_ready = sem("x2_ready")
        s_x2_mm = sem("x2_mm")
        s_x2_hi = sem("x2_hi")
        s_x2_lo = sem("x2_lo")
        s_x2_beta = sem("x2_beta")
        s_xl_mm = sem("xl_mm")
        s_xl_hi = sem("xl_hi")
        s_xl_lo = sem("xl_lo")
        s_ex_mm = sem("ex_mm")
        s_ex_hi = sem("ex_hi")
        s_ex_lo = sem("ex_lo")
        s_lg_mm = sem("lg_mm")
        s_lg_top = sem("lg_top")
        s_route = sem("route")
        s_up_mm = sem("up_mm")
        s_up_relu = sem("up_relu")
        s_up_sq = sem("up_sq")
        s_up_hi = sem("up_hi")
        s_up_lo = sem("up_lo")
        s_down_mm = sem("down_mm")
        s_r_mm = sem("r_mm")
        s_r_scaled = sem("r_scaled")
        s_u_ready = sem("u_ready")
        s_u_stats_a = sem("u_stats_a")
        s_u_stats_b = sem("u_stats_b")
        s_u_eps = sem("u_eps")
        s_u_rstd = sem("u_rstd")
        s_u_gamma = sem("u_gamma")
        s_w_sum = sem("w_sum")
        s_w_stats_a = sem("w_stats_a")
        s_w_stats_b = sem("w_stats_b")
        s_w_eps = sem("w_eps")
        s_w_rstd = sem("w_rstd")
        s_out_ready = sem("out_ready")
        s_landed = [sem(f"landed{i}") for i in range(SLOTS)]
        s_got = [[sem(f"got{hf}_{i}") for i in range(RING)] for hf in range(2)]
        s_bias_landed = [sem(f"bias_landed{i}") for i in range(2)]

        def due(count):
            return not isinstance(count, int) or count > 0

        block = ctx.enter_context(nc.Block())

        def flat(x):
            n = len(x.shape)
            return x if n == 2 else x.rearrange({3: "p a b -> p (a b)", 4: "p a b c -> p (a b c)",
                                                 5: "p a b c d -> p (a b c d)"}[n])

        dftC = [at[i].rearrange("p a b n -> p (a b) n") for i in (0, 1)]
        def dftX(i, hf):
            x = wqk[i].rearrange("p a b c n -> p (a b c n)") if hf == 0 else vv[i].rearrange("p b n -> p (b n)")
            return x.rearrange("p (c n) -> p c n", c=DC)
        dftD = [ext[i].rearrange("p a n -> p (a n)").rearrange("p (c n) -> p c n", c=DC) for i in (0, 1)]

        def sq(i):
            return xn[i][:, :, HALF:TOK]

        PC_INV = 4

        def dft_dst(i, piece):
            return (dftC[i][:, 0:2], dftX(i, 0)[:, 0:2], dftC[i][:, 2:4], dftX(i, 0)[:, 2:4], ext[i][:, :, :],
                    dftX(i, 1)[:, 0:2], dftX(i, 1)[:, 2:4])[piece]

        def shifted(n):
            return flat(smx[:, n % RING])

        def slot_at(w):
            return (DFT_PIECES + w) % SLOTS

        def landed_count(w):
            return 16 * ((DFT_PIECES + w) // SLOTS + 1)

        def raw2(slot):
            return raw[:, slot].rearrange("p (a n) -> p a n", a=2)

        def piece_qk(g, hp):
            if isinstance(g, int) and g == 0:
                return (PC_QK00, PC_QK01)[hp]
            return LOOP0 + 4 * (g - 1) + (0, 3)[hp]

        def piece_wv(g):
            if isinstance(g, int) and g == 0:
                return PC_WV0
            return LOOP0 + 4 * (g - 1) + 1

        def piece_wo(g):
            if isinstance(g, int) and g == PAIRS - 1:
                return LOOP0 + 4 * g
            return LOOP0 + 4 * g + 2

        def slot_of(w0, k):
            return (DFT_PIECES + LOOP0 + k) % SLOTS

        def rounds(g, k):
            return g + (DFT_PIECES + LOOP0 + k) // SLOTS + 1

        def nxt(g, j):
            return (g, j + 1) if j < 3 else (g + 1, 0)

        def every_pair(engine, body):
            body(0)
            with engine.Fori(1, PAIRS - 1) as g:
                body(g)
            body(PAIRS - 1)

        def heads_out(i, j):
            return at[i][:, j // 2, j % 2].rearrange("p (b n) -> p b n", b=HB)

        def is_last(g):
            return isinstance(g, int) and g == PAIRS - 1

        FFN0 = LOOP0 + 4 * (PAIRS - 1) + 1
        UP, FC1, EXPERT, FC2, DOWN = (0, 1, 2, 3), 4, 5, 6, (7, 8, 9, 10)
        BY_VECTOR = (1, 3, 5, 6, 8, 10)
        expert = [flat(pt[i]).rearrange("p (c n) -> p c n", c=LC) for i in (0, 1)]
        wdown = [[flat(wqk[i]).rearrange("p (c n) -> p c n", c=4), flat(vv[i]).rearrange("p (c n) -> p c n", c=4)]
                 for i in (0, 1)]
        GX = LC * LAT + DC * NE

        def ffn_dst(i, k):
            if k in UP:
                return cx[i][:, k]
            if k == FC1:
                return flat(wv[i])
            if k == EXPERT:
                return flat(pt[i])
            if k == FC2:
                return flat(ext[i])
            d = k - DOWN[0]
            return flat(wdown[i][d // 2][:, 2 * (d % 2):2 * (d % 2) + 2, :])

        def ffn_src(k):
            return raw[:, (DFT_PIECES + FFN0 + k) % SLOTS, 0:LC * LAT if k == EXPERT else PIECE]

        def low_done(k):
            if k < 0:
                return s_dft_lo, k + DFT_PIECES + 1
            if k in (PC_WV0, PC_QK00, PC_QK01):
                return s_first_lo, k - PC_WV0 + 1
            if k < CTX_PIECES:
                return s_w_lo, k + 1
            if k < FFN0:
                return s_w_lo, k - 2
            f = k - FFN0
            if f in BY_VECTOR:
                return s_f_lo, BY_VECTOR.index(f) + 1
            return s_w_lo, k - 2 - len([b for b in BY_VECTOR if b < f])

        def hidden(i, c):
            return at[i][:, (c % 4) // 2, c % 2]

        def tile_cols(tile):
            return slice(tile * P, (tile + 1) * P)

        def half_cols(hf):
            return slice(hf * HALF, (hf + 1) * HALF)

        @block.sync
        def _(sp):
            def stage(piece, src):
                old = piece - SLOTS - DFT_PIECES
                if isinstance(old, int):
                    if old + DFT_PIECES >= 0:
                        sp.wait_ge(*low_done(old))
                    if old == FFN0 + EXPERT:
                        sp.wait_ge(s_gate_lo, 1)
                else:
                    sp.wait_ge(s_w_lo, old - 2)
                return src

            def load(piece, slot, src):
                stage(piece, src)
                sp.dma_start(raw[:, slot, 0:src.shape[1]], src).then_inc(s_landed[slot], 16)

            def load_rows(hf):
                sp.dma_start(acc[:, HB * hf:HB * hf + HB, :],
                             t["x"].rearrange("(b p) d -> p b d", p=P)[:, HB * hf:HB * hf + HB, :]
                             ).then_inc(s_x_landed, 16)

            for p in range(DFT_PIECES):
                load(p, p % SLOTS, t["dft"][p])
                if p == PC_INV - 1:
                    sp.dma_start(m8[:, :, :], t["mask"].rearrange("b q k -> q b k")).then_inc(s_mask_landed, 16)
                if p == PC_INV:
                    load_rows(0)
            load_rows(1)
            sp.dma_start(lnw[:, :], t["ln_w"].partition_broadcast(P)).then_inc(s_lnw_landed, 16)
            for c in range(CTX_PIECES):
                load(DFT_PIECES + c, slot_at(c), t["ctxT"][c])


            def load_bias(g, hp):
                if due(4 * g - 1 + hp):
                    sp.wait_ge(s_bm_ready, 4 * g - 1 + hp)
                sp.dma_start(bias[:, hp, :], row(t["bias"], 2 * g + hp)).then_inc(s_bias_landed[hp], 16)

            def row(x, i):
                return x[i] if isinstance(i, int) else x[bass.ds(i, 1)].rearrange("o p n -> (o p) n")

            load(DFT_PIECES + PC_WV0, slot_at(PC_WV0), t["wv"][0])
            for hp in range(2):
                load_bias(0, hp)
                pc = DFT_PIECES + (PC_QK00, PC_QK01)[hp]
                load(pc, pc % SLOTS, t["wqk"][hp])

            def pair_loads(g):
                base = DFT_PIECES + LOOP0 + 4 * g
                if is_last(g):
                    load(base, slot_of(g, 0), row(t["wo"], g))
                    return
                load(base, slot_of(g, 0), row(t["wqk"], 2 * g + 2))
                load(base + 1, slot_of(g, 1), row(t["wv"], g + 1))
                load(base + 2, slot_of(g, 2), row(t["wo"], g))
                load_bias(g + 1, 0)
                load(base + 3, slot_of(g, 3), row(t["wqk"], 2 * g + 3))
                load_bias(g + 1, 1)

            every_pair(sp, pair_loads)

            sp.wait_ge(s_xt_mm, B)
            sp.dma_start(rows[:, 0], t["gamma"].partition_broadcast(P)).then_inc(s_rows_landed, 16)
            sp.dma_start(rows[:, 1], t["beta"].partition_broadcast(P)).then_inc(s_rows_landed, 16)
            for k in range(FFN_PIECES):
                pc = DFT_PIECES + FFN0 + k
                load(pc, pc % SLOTS, t["gx"] if k == EXPERT else t["ffn"][k - (k > EXPERT)])
            for tile in range(B):
                sp.wait_ge(s_out_ready, tile + 1)
                sp.dma_start(t["out"][tile_cols(tile), :], acc[:, tile, :]).then_inc(s_stored, 16)
            sp.wait_ge(s_stored, 16 * B)

        @block.gpsimd
        def _(pool):
            g = nc.gpsimd
            g.memset(half_pow[:, :], -0.5).then_inc(s_consts, 1)
            g.iota(rowbase[:, :], [[0, 1]], base=1, channel_multiplier=2 * D,
                   allow_small_or_imprecise_dtypes=True).then_inc(s_consts, 1)
            g.memset(ident[:, :], 0.0).then_inc(s_consts, 1)
            pool.wait_ge(s_consts, 3)
            g.affine_select(out=ident[:, :], in_=ident[:, :], compare_op=ALU.not_equal, fill=1.0, base=0,
                            pattern=[[-1, P]], channel_multiplier=1).then_inc(s_consts, 1)
            g.memset(ones[:, :], 1.0).then_inc(s_consts, 1)

            def split_lo(w, src, dst_hi, dst_lo):
                pool.wait_ge(s_w_hi, w + 1)
                g.tensor_tensor(dst_lo, src, dst_hi, ALU.subtract).then_inc(s_w_lo, 1)

            def shifted_rows(hf):
                pool.wait_ge(s_general, hf + 1)
                count = pool.value_load(general[0:1, hf:hf + 1], min_val=0, max_val=1)
                with pool.If(count != 0):
                    for n in range(HB * (LAGS - 1)):
                        tile, k = HB * hf + n // (LAGS - 1), n % (LAGS - 1)
                        if n >= RING:
                            pool.wait_ge(s_acc_sum[hf], n - RING + 1)
                        g.indirect_dma_start(shifted(n), None, t["xx"],
                                             bass.IndirectOffsetOnAxis(ap=gidx[:, tile, k:k + 1], axis=0)
                                             ).then_inc(s_got[hf][n % RING], 16)
                    pool.wait_ge(s_acc_sum[hf], HB * (LAGS - 1))

            def factors(hf):
                pool.wait_ge(s_stats_b, HB * hf + HB)
                cols, n0 = slice(HB * hf, HB * hf + HB), 6 * hf
                var = mv[:, cols, 1]
                r, powers = prep[:, 1, cols], half_pow[:, 0:1].to_broadcast([P, HB])
                g.tensor_scalar(prep[:, 0, cols], var, EPS, None, ALU.add).then_inc(s_prep, 1)
                pool.wait_ge(s_prep, n0 + 1)
                g.tensor_tensor(r, prep[:, 0, cols], powers, ALU.pow).then_inc(s_prep, 1)
                pool.wait_ge(s_prep, n0 + 2)
                g.tensor_tensor(prep[:, 2, cols], var, r, ALU.mult).then_inc(s_prep, 1)
                pool.wait_ge(s_prep, n0 + 3)
                g.tensor_tensor(prep[:, 2, cols], prep[:, 2, cols], r, ALU.mult).then_inc(s_prep, 1)
                pool.wait_ge(s_prep, n0 + 4)
                g.tensor_scalar(prep[:, 3, cols], prep[:, 2, cols], EPS, None, ALU.add).then_inc(s_prep, 1)
                pool.wait_ge(s_prep, n0 + 5)
                g.tensor_tensor(prep[:, 4, cols], prep[:, 3, cols], powers, ALU.pow).then_inc(s_prep, 1)

            def ctx_lo(c):
                split_lo(c, raw[:, slot_at(c)], cx[0][:, c], cx[1][:, c])

            shifted_rows(0)
            factors(0)
            for c in range(CTX_PIECES):
                ctx_lo(c)
            shifted_rows(1)
            factors(1)


            def bias_and_mask(n, g, j):
                hp, hf = j % 2, j // 2
                pool.wait_ge(s_bias_landed[hp], 16 * (g + 1))
                if due(n):
                    pool.wait_ge(s_scores_sum, n)
                if isinstance(n, int) and n == 0:
                    pool.wait_ge(s_far_ready, 1)
                g_ = bias[:, hp:hp + 1, :].to_broadcast([P, HB, P])
                nc.gpsimd.tensor_tensor(bm, far[:, HB * hf:HB * hf + HB, :], g_, ALU.add).then_inc(s_bm_ready, 1)

            wflat = [(flat(wv[0]), flat(wv[1])), (flat(wqk[0][:, 0]), flat(wqk[1][:, 0])),
                     (flat(wqk[0][:, 1]), flat(wqk[1][:, 1])), (flat(wo[0]), flat(wo[1]))]
            WV, WQ0, WQ1, WO = range(4)

            bias_and_mask(0, 0, 0)

            def pair_pool(g):
                last = is_last(g)
                for j in range(4):
                    n = 4 * g + j
                    if not (last and j == 3):
                        bias_and_mask(n + 1, *nxt(g, j))
                    if j == 1 and not last:
                        split_lo(piece_qk(g + 1, 0), raw[:, slot_of(g, 0)], *wflat[WQ0])
                        split_lo(piece_wv(g + 1), raw[:, slot_of(g, 1)], *wflat[WV])
                    if j == 2:
                        split_lo(piece_wo(g), raw[:, slot_of(g, 0 if last else 2)], *wflat[WO])
                        if not last:
                            split_lo(piece_qk(g + 1, 1), raw[:, slot_of(g, 3)], *wflat[WQ1])

            every_pair(pool, pair_pool)

            def power(s_eps, s_out, var, mid, dst, tile):
                g = nc.gpsimd
                g.tensor_scalar(mid, var, EPS, None, ALU.add).then_inc(s_eps, 1)
                pool.wait_ge(s_eps, tile + 1)
                g.tensor_tensor(dst, mid, half_pow[:, :], ALU.pow).then_inc(s_out, 1)

            def ffn_lo(k):
                if k not in BY_VECTOR:
                    split_low(k)

            def split_low(k):
                pool.wait_ge(s_w_hi, FFN0 + k + 1)
                nc.gpsimd.tensor_tensor(ffn_dst(1, k), ffn_src(k), ffn_dst(0, k), ALU.subtract
                                        ).then_inc(s_w_lo, 1)

            def y_power(tile):
                pool.wait_ge(s_y_stats_b, tile + 1)
                power(s_y_eps, s_y_rstd, mv[:, tile, 1:2], stat[:, tile, 0:1], stat[:, tile, 1:2], tile)

            def add_beta(tile):
                pool.wait_ge(s_x2_mm, tile + 1)
                if tile == 0:
                    pool.wait_ge(s_rows_landed, 32)
                nc.gpsimd.tensor_tensor(acc[:, tile, :], acc[:, tile, :], rows[:, 1], ALU.add
                                        ).then_inc(s_x2_beta, 1)

            def u_power(tile):
                pool.wait_ge(s_u_stats_b, tile + 1)
                power(s_u_eps, s_u_rstd, mv[:, tile, 1:2], stat[:, tile, 0:1], stat[:, tile, 1:2], tile)

            def w_power(tile):
                pool.wait_ge(s_w_stats_b, tile + 1)
                power(s_w_eps, s_w_rstd, mv[:, tile, 1:2], stat[:, tile, 2:3], stat[:, tile, 3:4], tile)

            for tile in range(HB):
                y_power(tile)
                if tile % 2:
                    ffn_lo(tile - 1)
            ffn_lo(FC1)
            for tile in range(HB, B):
                y_power(tile)
            ffn_lo(DOWN[0])
            ffn_lo(DOWN[2])
            for tile in range(HB):
                add_beta(tile)
            for tile in range(HB):
                u_power(tile)
            for tile in range(HB):
                w_power(tile)
            for tile in range(HB, B):
                add_beta(tile)
            for tile in range(HB, B):
                u_power(tile)
                w_power(tile)

        @block.scalar
        def _(act):
            a = nc.scalar

            def copy_hi(dst, src):
                return a.activation(dst, src, ACT.Copy)

            def dft_hi(p):
                act.wait_ge(s_landed[p % SLOTS], 16 * (p // SLOTS + 1))
                copy_hi(dft_dst(0, p), raw2(p % SLOTS)).then_inc(s_dft_hi, 1)

            def square(hf, j):
                n = 4 * hf + j
                act.wait_ge(s_dft_mm, n + 1)
                a.activation(banks[j][:, :], banks[j][:, :], ACT.Square).then_inc(s_sq_done, 1)
                act.wait_ge(s_sq_done, n + 1)
                if j == 0 and hf == 1:
                    act.wait_ge(s_corr_mm, HB)
                copy_hi(sq(0)[:, j], banks[j][:, :]).then_inc(s_sq_hi, 1)

            def lag0(tile):
                if tile == 0:
                    act.wait_ge(s_x_landed, 16)
                if tile == HB:
                    act.wait_ge(s_x_landed, 32)
                act.wait_ge(s_sq_done, 4 * (tile // HB) + 4)
                if due(tile):
                    act.wait_ge(s_lag0, tile)
                a.activation(flat(wv[1][:, 0:2]), acc[:, tile, :], ACT.Square, accum_out=topv[:, tile, 0:1]
                             ).then_inc(s_lag0, 1)

            def mirror(tile):
                bank = banks[4 + tile % 4]
                act.wait_ge(s_corr_mm, tile + 1)
                a.activation(bank[:, LAST_LAG:D - 1], bank[:, 0:LAST_LAG - 1][:, ::-1], ACT.Copy
                             ).then_inc(s_mirrored, 1)

            def weigh(tile):
                act.wait_ge(s_top_max, 2 * tile + 2)
                a.activation(wts[:, tile, 0:LAGS], topv[:, tile, 0:LAGS], ACT.Exp, bias=topm[:, tile, 1:2],
                             accum_out=wsum[:, tile, 0:1]).then_inc(s_w_exp, 1)

            def scale_rows(tile):
                act.wait_ge(s_w0_ready, tile + 1)
                a.activation(acc[:, tile, :], acc[:, tile, :], ACT.Copy, scale=wsum[:, tile, 1:2]
                             ).then_inc(s_acc_scaled, 1)

            def double(tile):
                act.wait_ge(s_xn_ready, tile + 1)
                a.activation(acc[:, tile, :], acc[:, tile, :], ACT.Copy, scale=2.0).then_inc(s_acc_x1, 1)

            def xt_hi(tile):
                act.wait_ge(s_xt_mm, tile + 1)
                if tile == HB:
                    act.wait_ge(s_corr_mm, B)
                copy_hi(xn[0][:, :, tile * P:(tile + 1) * P], banks[2 + 2 * (tile % 2)][:, :].rearrange(
                    "p (c n) -> p c n", c=DC)).then_inc(s_xt_hi, 1)

            def ctx_hi(c):
                act.wait_ge(s_landed[slot_at(c)], landed_count(c))
                copy_hi(cx[0][:, c], raw[:, slot_at(c)]).then_inc(s_w_hi, 1)

            for p in range(PC_INV + 1):
                dft_hi(p)
            for j in range(4):
                square(0, j)
                if j >= 2:
                    dft_hi(PC_INV + j - 1)
            for tile in range(HB):
                lag0(tile)
                mirror(tile)
                if tile >= 1:
                    weigh(tile - 1)
                    scale_rows(tile - 1)
            weigh(HB - 1)
            scale_rows(HB - 1)
            for j in range(4):
                square(1, j)
            for tile in range(HB, B):
                ctx_hi(tile - HB)
                lag0(tile)
                mirror(tile)
                double(tile - HB)
                xt_hi(tile - HB)
                if tile > HB:
                    weigh(tile - 1)
                    scale_rows(tile - 1)
            weigh(B - 1)
            scale_rows(B - 1)


            def weight_hi(dst, slot, count):
                act.wait_ge(s_landed[slot], 16 * count)
                copy_hi(dst, raw[:, slot]).then_inc(s_w_hi, 1)

            def hi_of(s_mm, s_hi, count, dst, src):
                act.wait_ge(s_mm, count)
                copy_hi(dst, src).then_inc(s_hi, 1)

            def value_dst(i, m):
                t0 = 2 * (m % 4)
                return vv[i][:, t0:t0 + 2, :]

            def exps_of(n):
                act.wait_ge(s_max_neg, n + 1)
                if due(n):
                    act.wait_ge(s_probs_ready, n)
                for b in range(HB):
                    a.activation(exps[:, b, :], scores_sb[:, b, :], ACT.Exp, bias=nmax[:, 1, b:b + 1],
                                 accum_out=esum[:, 0, b:b + 1]).then_inc(s_exp_done, 1)

            for w, dst in ((PC_WV0, flat(wv[0])), (PC_QK00, flat(wqk[0][:, 0])), (PC_QK01, flat(wqk[0][:, 1]))):
                act.wait_ge(s_landed[slot_at(w)], landed_count(w))
                copy_hi(dst, raw[:, slot_at(w)]).then_inc(s_w_hi, 1)
            hi_of(s_k_mm, s_k_hi, 1, qk[0][:, 1], psK[:, :])
            hi_of(s_v_mm, s_v_hi, 1, value_dst(0, 0), psV[:, :].rearrange("p (b n) -> p b n", b=2))
            hi_of(s_q_mm, s_q_hi, 1, qk[0][:, 0], psQ[:, :])
            hi_of(s_v_mm, s_v_hi, 2, value_dst(0, 1), psV[:, :].rearrange("p (b n) -> p b n", b=2))
            exps_of(0)
            for tile in range(HB, B):
                double(tile)
                xt_hi(tile)

            def ffn_hi(k):
                pc = DFT_PIECES + FFN0 + k
                act.wait_ge(s_landed[pc % SLOTS], 16 * (pc // SLOTS + 1))
                if k in UP or k in DOWN[:2]:
                    act.wait_ge(s_k_mm, units)
                if k in UP or k == FC1:
                    act.wait_ge(s_v_mm, units)
                if k == EXPERT or k in DOWN[2:]:
                    act.wait_ge(s_a_mm, units)
                copy_hi(ffn_dst(0, k), ffn_src(k)).then_inc(s_w_hi, 1)
                if k == EXPERT:
                    copy_hi(flat(gate[0]), raw[:, pc % SLOTS, LC * LAT:GX]).then_inc(s_gate_hi, 1)

            def pair_act(g):
                last = is_last(g)
                for j in range(4):
                    n = 4 * g + j
                    if j == 2:
                        k = 0 if last else 2
                        if due(8 * g):
                            act.wait_ge(s_o_mm, 8 * g)
                        weight_hi(flat(wo[0]), slot_of(g, k), rounds(g, k))
                    front = not (last and j == 3)
                    if front:
                        act.wait_ge(s_scores_mm, n + 1)
                        hi_of(s_q_mm, s_q_hi, n + 2, qk[0][:, 0], psQ[:, :])
                        hi_of(s_k_mm, s_k_hi, n + 2, qk[0][:, 1], psK[:, :])
                    if due(n):
                        act.wait_ge(s_a_mm, n)
                    hi_of(s_t_mm, s_t_hi, n + 1, flat(pt[0]), psT[:, :])
                    if j == 1 and not last:
                        act.wait_ge(s_k_mm, 4 * g + 3)
                        weight_hi(flat(wqk[0][:, 0]), slot_of(g, 0), rounds(g, 0))
                    if j == 2 and not last:
                        act.wait_ge(s_k_mm, 4 * g + 4)
                        weight_hi(flat(wqk[0][:, 1]), slot_of(g, 3), rounds(g, 3))
                    if not (last and j >= 2):
                        if due(n - (1 if j % 2 else 0)):
                            act.wait_ge(s_a_mm, n - (1 if j % 2 else 0))
                        hi_of(s_v_mm, s_v_hi, n + 3, value_dst(0, j + 2), psV[:, :].rearrange("p (b n) -> p b n", b=2))
                    if j == 1 and not last:
                        act.wait_ge(s_v_mm, 4 * g + 4)
                        weight_hi(flat(wv[0]), slot_of(g, 1), rounds(g, 1))
                    if due(8 * g - 4 + (4 if j >= 2 else 0)):
                        act.wait_ge(s_o_mm, 8 * g - 4 + (4 if j >= 2 else 0))
                    hi_of(s_a_mm, s_a_hi, n + 1, heads_out(0, j), psA[:, :, 0])
                    if front:
                        exps_of(n + 1)
                    if last and j == 2:
                        for k in (0, 1):
                            ffn_hi(k)
                    if last and j == 3:
                        for k in (2, 3, 4):
                            ffn_hi(k)

            every_pair(act, pair_act)

            def x2_hi(tile):
                act.wait_ge(s_x2_mm, tile + 1)
                if tile == 0:
                    act.wait_ge(s_q_mm, units)
                copy_hi(xn[0][:, :, tile_cols(tile)], banks[2 + tile % 2][:, :].rearrange("p (c n) -> p c n", c=DC)
                        ).then_inc(s_x2_hi, 1)

            def product_hi(s_mm, s_hi, hf, c, dst):
                act.wait_ge(s_mm, 2 * hf + c + 1)
                copy_hi(dst, banks[2 + c][:, :]).then_inc(s_hi, 1)

            def up_act(hf, c):
                n, bank = IC * hf + c, banks[c % 2]
                act.wait_ge(s_up_mm, n + 1)
                a.activation(bank[:, :], bank[:, :], ACT.Relu).then_inc(s_up_relu, 1)
                act.wait_ge(s_up_relu, n + 1)
                a.activation(bank[:, :], bank[:, :], ACT.Square).then_inc(s_up_sq, 1)
                act.wait_ge(s_up_sq, n + 1)
                if due(n - 3):
                    act.wait_ge(s_down_mm, n - 3)
                if n == 0:
                    act.wait_ge(s_o_mm, 2 * units)
                copy_hi(hidden(0, c), bank[:, :]).then_inc(s_up_hi, 1)

            def routed_scale(tile):
                act.wait_ge(s_r_mm, tile + 1)
                act.wait_ge(s_route, tile + 1)
                if due(tile - 3):
                    act.wait_ge(s_w_sum, tile - 3)
                a.activation(flat(smx[:, tile % 4]), banks[tile % 2][:, :], ACT.Copy, scale=rsum[:, tile, :]
                             ).then_inc(s_r_scaled, 1)

            for k in (EXPERT, FC2):
                ffn_hi(k)
            for tile in range(HB):
                x2_hi(tile)
            for hf in range(2):
                if due(2 * hf):
                    act.wait_ge(s_ex_mm, 2 * hf)
                for c in range(LC):
                    product_hi(s_xl_mm, s_xl_hi, hf, c, qk[0][:, c])
                up_act(hf, 0)
                if hf == 0:
                    ffn_hi(DOWN[0])
                up_act(hf, 1)
                if due(HB * hf):
                    act.wait_ge(s_r_mm, HB * hf)
                for c in range(LC):
                    product_hi(s_ex_mm, s_ex_hi, hf, c, wo[0][:, c])
                for c in range(2, IC):
                    if hf == 0 and c < 5:
                        ffn_hi(DOWN[c - 1])
                    up_act(hf, c)
                if hf == 0:
                    for tile in range(HB, B):
                        x2_hi(tile)
                for tile in range(HB * hf, HB * hf + HB):
                    routed_scale(tile)

        @block.vector
        def _(dve):
            v = nc.vector

            def lo_part(dst, src, hi):
                return v.tensor_tensor(dst, src, hi, ALU.subtract)

            def dft_lo(p):
                dve.wait_ge(s_dft_hi, p + 1)
                lo_part(dft_dst(1, p), raw2(p % SLOTS), dft_dst(0, p)).then_inc(s_dft_lo, 1)

            def square_lo(hf, j):
                dve.wait_ge(s_sq_hi, 4 * hf + j + 1)
                lo_part(sq(1)[:, j], banks[j][:, :], sq(0)[:, j]).then_inc(s_sq_lo, 1)

            def top(tile):
                corr = banks[4 + tile % 4]
                dve.wait_ge(s_mirrored, tile + 1)
                v.max(topv[:, tile, 1:9], corr[:, 0:D - 1]).then_inc(s_top_val, 1)
                dve.wait_ge(s_top_val, tile + 1)
                dve.wait_ge(s_lag0, tile + 1)
                v.tensor_reduce(topm[:, tile, 0:1], topv[:, tile, 0:LAGS], AX.X, ALU.max).then_inc(s_top_max, 1)
                v.max_index(topi[:, tile, :], topv[:, tile, 1:9], corr[:, 0:D - 1]).then_inc(s_top_idx, 1)
                dve.wait_ge(s_top_max, 2 * tile + 1)
                v.tensor_scalar(topm[:, tile, 1:2], topm[:, tile, 0:1], -1.0, None, ALU.mult).then_inc(s_top_max, 1)
                dve.wait_ge(s_top_idx, tile + 1)
                v.tensor_scalar(gidx[:, tile, :], topi[:, tile, :], rowbase[:, :], float(tile * P * 2 * D),
                                ALU.add, ALU.add).then_inc(s_gather_idx, 1)

            def weights(tile):
                dve.wait_ge(s_w_exp, tile + 1)
                v.reciprocal(topm[:, tile, 2:3], wsum[:, tile, 0:1]).then_inc(s_w_rec, 1)
                dve.wait_ge(s_w_rec, tile + 1)
                v.tensor_scalar(wsum[:, tile, 1:2], wts[:, tile, 0:1], topm[:, tile, 2:3], 1.0, ALU.mult, ALU.add
                                ).then_inc(s_w0_ready, 1)
                v.tensor_scalar(wts[:, tile, 1:LAGS], wts[:, tile, 1:LAGS], topm[:, tile, 2:3], None, ALU.mult
                                ).then_inc(s_w_ready, 1)

            def other_weights(hf):
                dve.wait_ge(s_w_ready, HB * hf + HB)
                v.tensor_reduce(others[:, hf:hf + 1], wts[:, HB * hf:HB * hf + HB, 1:LAGS], AX.XY, ALU.add
                                ).then_inc(s_others, 1)
                dve.wait_ge(s_others, hf + 1)
                v.tensor_scalar(nonzero[:, hf:hf + 1], others[:, hf:hf + 1], 0.0, None, ALU.not_equal
                                ).then_inc(s_nonzero, 1)

            def delays_sum(hf):
                dve.wait_ge(s_count_mm, hf + 1)
                v.tensor_scalar(general[0:1, hf:hf + 1], banks[4 + hf][0:1, 0:1], 0.0, None,
                                ALU.not_equal).then_inc(s_general, 1)
                dve.wait_ge(s_general, hf + 1)
                dve.wait_ge(s_acc_scaled, HB * hf + HB)
                dve.wait_ge(s_gather_idx, HB * hf + HB)
                count = dve.value_load(general[0:1, hf:hf + 1], min_val=0, max_val=1)
                with dve.If(count != 0):
                    for n in range(HB * (LAGS - 1)):
                        tile, k = HB * hf + n // (LAGS - 1), n % (LAGS - 1)
                        dve.wait_ge(s_got[hf][n % RING], 16 * (n // RING + 1))
                        if n % (LAGS - 1):
                            dve.wait_ge(s_acc_sum[hf], n)
                        v.scalar_tensor_tensor(acc[:, tile, :], shifted(n), wts[:, tile, k + 1:k + 2],
                                               acc[:, tile, :], ALU.mult, ALU.add).then_inc(s_acc_sum[hf], 1)
                    dve.wait_ge(s_acc_sum[hf], HB * (LAGS - 1))

            def stats(tile):
                v.bn_stats(st6[:, tile, :], acc[:, tile, :]).then_inc(s_stats_a, 1)
                dve.wait_ge(s_stats_a, tile + 1)
                v.bn_aggr(mv[:, tile, :], st6[:, tile, :]).then_inc(s_stats_b, 1)

            def norms(tile):
                if tile % HB == 0:
                    dve.wait_ge(s_prep, 6 * (tile // HB) + 6)
                if tile == 0:
                    dve.wait_ge(s_lnw_landed, 16)
                v.tensor_scalar(acc[:, tile, :], acc[:, tile, :], mv[:, tile, 0:1], prep[:, 1, tile:tile + 1],
                                ALU.subtract, ALU.mult).then_inc(s_x1_ready, 1)
                dve.wait_ge(s_x1_ready, tile + 1)
                if due(tile - 1):
                    dve.wait_ge(s_xt_mm, tile - 1)
                v.scalar_tensor_tensor(rows[:, tile % 2], acc[:, tile, :], prep[:, 4, tile:tile + 1], lnw[:, :],
                                       ALU.mult, ALU.mult).then_inc(s_xn_ready, 1)

            def xt_lo(tile):
                dve.wait_ge(s_xt_hi, tile + 1)
                part = slice(tile * P, (tile + 1) * P)
                lo_part(xn[1][:, :, part], banks[2 + 2 * (tile % 2)][:, :].rearrange("p (c n) -> p c n", c=DC),
                        xn[0][:, :, part]).then_inc(s_xt_lo, 1)

            for p in range(PC_INV):
                dft_lo(p)
            dve.wait_ge(s_consts, 5)
            dve.wait_ge(s_mask_landed, 16)
            v.tensor_scalar(far[:, :, :], m8[:, :, :], -1.0, FAR, ALU.add, ALU.mult).then_inc(s_far_ready, 1)
            dft_lo(PC_INV)
            for j in range(4):
                square_lo(0, j)
                if j >= 2:
                    dft_lo(PC_INV + j - 1)
            for tile in range(HB):
                top(tile)
                if tile >= 1:
                    weights(tile - 1)
            weights(HB - 1)
            other_weights(0)
            square_lo(1, 0)
            square_lo(1, 1)
            delays_sum(0)
            for tile in range(HB):
                stats(tile)
            square_lo(1, 2)
            square_lo(1, 3)
            for tile in range(HB, B):
                norms(tile - HB)
                top(tile)
                xt_lo(tile - HB)
                if tile > HB:
                    weights(tile - 1)
            weights(B - 1)
            other_weights(1)


            def lo_of(s_hi, s_lo, count, dst, src, hi):
                dve.wait_ge(s_hi, count)
                lo_part(dst, src, hi).then_inc(s_lo, 1)

            def value_dst(i, m):
                t0 = 2 * (m % 4)
                return vv[i][:, t0:t0 + 2, :]

            def softmax_in(n):
                dve.wait_ge(s_scores_mm, n + 1)
                dve.wait_ge(s_bm_ready, n + 1)
                if due(4 * n):
                    dve.wait_ge(s_exp_done, 4 * n)
                v.tensor_tensor(scores_sb, psS[:, :, 0], bm, ALU.add).then_inc(s_scores_sum, 1)
                dve.wait_ge(s_scores_sum, n + 1)
                v.tensor_tensor(scores_sb, psS[:, :, 1], scores_sb, ALU.add).then_inc(s_scores_full, 1)
                dve.wait_ge(s_scores_full, n + 1)
                v.tensor_reduce(nmax[:, 0, :], scores_sb, AX.X, ALU.max).then_inc(s_scores_max, 1)
                dve.wait_ge(s_scores_max, n + 1)
                v.tensor_scalar(nmax[:, 1, :], nmax[:, 0, :], -0.5 * FAR, -1.0, ALU.max, ALU.mult
                                ).then_inc(s_max_neg, 1)

            def softmax_out(n):
                dve.wait_ge(s_exp_done, 4 * n + 4)
                v.tensor_scalar(esum[:, 1, :], esum[:, 0, :], 1e-30, None, ALU.max).then_inc(s_sum_clamped, 1)
                dve.wait_ge(s_sum_clamped, n + 1)
                v.reciprocal(esum[:, 2, :], esum[:, 1, :]).then_inc(s_sum_inverse, 1)
                dve.wait_ge(s_sum_inverse, n + 1)
                if due(n):
                    dve.wait_ge(s_t_mm, n)
                v.tensor_tensor(probs, exps, esum[:, 2, :].unsqueeze(2).to_broadcast([P, HB, P]), ALU.mult
                                ).then_inc(s_probs_ready, 1)

            def attended(n, j):
                dve.wait_ge(s_a_hi, n + 1)
                v.tensor_tensor(rest[:, :, :], psA[:, :, 0], heads_out(0, j), ALU.subtract).then_inc(s_a_rest, 1)
                dve.wait_ge(s_a_rest, n + 1)
                v.tensor_tensor(heads_out(1, j), psA[:, :, 1], rest[:, :, :], ALU.add).then_inc(s_a_lo, 1)

            def add_out(o, i, tile, src=psO):
                dve.wait_ge(s_o_mm, 2 * o + i + 1)
                v.tensor_tensor(acc[:, tile, :], src[i][:, :], acc[:, tile, :], ALU.add).then_inc(s_o_add, 1)

            def first_lo(w, dst_hi, dst_lo):
                dve.wait_ge(s_w_hi, w + 1)
                lo_part(dst_lo, raw[:, slot_at(w)], dst_hi).then_inc(s_first_lo, 1)

            first_lo(PC_WV0, flat(wv[0]), flat(wv[1]))
            first_lo(PC_QK00, flat(wqk[0][:, 0]), flat(wqk[1][:, 0]))
            delays_sum(1)
            for tile in range(HB, B):
                stats(tile)
            first_lo(PC_QK01, flat(wqk[0][:, 1]), flat(wqk[1][:, 1]))
            lo_of(s_k_hi, s_k_lo, 1, qk[1][:, 1], psK[:, :], qk[0][:, 1])
            lo_of(s_v_hi, s_v_lo, 1, value_dst(1, 0), psV[:, :].rearrange("p (b n) -> p b n", b=2), value_dst(0, 0))
            lo_of(s_q_hi, s_q_lo, 1, qk[1][:, 0], psQ[:, :], qk[0][:, 0])
            lo_of(s_v_hi, s_v_lo, 2, value_dst(1, 1), psV[:, :].rearrange("p (b n) -> p b n", b=2), value_dst(0, 1))
            softmax_in(0)
            norms(HB)
            softmax_out(0)
            norms(HB + 1)
            xt_lo(HB)
            norms(HB + 2)
            xt_lo(HB + 1)
            norms(HB + 3)
            xt_lo(HB + 2)
            xt_lo(HB + 3)

            def pair_dve(g):
                last = is_last(g)
                for j in range(4):
                    n = 4 * g + j
                    front = not (last and j == 3)
                    if front:
                        lo_of(s_q_hi, s_q_lo, n + 2, qk[1][:, 0], psQ[:, :], qk[0][:, 0])
                        lo_of(s_k_hi, s_k_lo, n + 2, qk[1][:, 1], psK[:, :], qk[0][:, 1])
                    lo_of(s_t_hi, s_t_lo, n + 1, flat(pt[1]), psT[:, :], flat(pt[0]))
                    if not (last and j >= 2):
                        lo_of(s_v_hi, s_v_lo, n + 3, value_dst(1, j + 2), psV[:, :].rearrange("p (b n) -> p b n", b=2),
                              value_dst(0, j + 2))
                    attended(n, j)
                    if front:
                        softmax_in(n + 1)
                    if not (isinstance(g, int) and g == 0 and j < 2):
                        for i in range(2):
                            add_out(n - 2, i, (2 * ((j + 2) % 4) + i) % B)
                            if front and i == 0:
                                softmax_out(n + 1)
                    elif front:
                        softmax_out(n + 1)

            every_pair(dve, pair_dve)

            def ffn_lo(k):
                dve.wait_ge(s_w_hi, FFN0 + k + 1)
                lo_part(ffn_dst(1, k), ffn_src(k), ffn_dst(0, k)).then_inc(s_f_lo, 1)
                if k == EXPERT:
                    dve.wait_ge(s_gate_hi, 1)
                    slot = (DFT_PIECES + FFN0 + k) % SLOTS
                    lo_part(flat(gate[1]), raw[:, slot, LC * LAT:GX], flat(gate[0])).then_inc(s_gate_lo, 1)

            def y_stats(tile):
                dve.wait_ge(s_o_add, 2 * (units - 4) + tile + 1)
                v.bn_stats(st6[:, tile, :], acc[:, tile, :]).then_inc(s_y_stats_a, 1)
                dve.wait_ge(s_y_stats_a, tile + 1)
                v.bn_aggr(mv[:, tile, :], st6[:, tile, :]).then_inc(s_y_stats_b, 1)

            def x2(tile):
                dve.wait_ge(s_y_rstd, tile + 1)
                v.tensor_scalar(acc[:, tile, :], acc[:, tile, :], mv[:, tile, 0:1], stat[:, tile, 1:2],
                                ALU.subtract, ALU.mult).then_inc(s_x2_ready, 1)

            def x2_lo(tile):
                dve.wait_ge(s_x2_hi, tile + 1)
                lo_part(xn[1][:, :, tile_cols(tile)], banks[2 + tile % 2][:, :].rearrange("p (c n) -> p c n", c=DC),
                        xn[0][:, :, tile_cols(tile)]).then_inc(s_x2_lo, 1)

            def product_lo(s_hi, s_lo, hf, c, dst):
                dve.wait_ge(s_hi, 2 * hf + c + 1)
                lo_part(dst[1][:, c], banks[2 + c][:, :], dst[0][:, c]).then_inc(s_lo, 1)

            def up_lo(hf, c):
                dve.wait_ge(s_up_hi, IC * hf + c + 1)
                lo_part(hidden(1, c), banks[c % 2][:, :], hidden(0, c)).then_inc(s_up_lo, 1)

            def route(hf):
                dve.wait_ge(s_lg_mm, hf + 1)
                for i in range(HB):
                    v.max(lg8[:, HB * hf + i, :], banks[2][:, i * NE:(i + 1) * NE]).then_inc(s_lg_top, 1)
                dve.wait_ge(s_lg_top, HB * hf + HB)
                for i in range(HB):
                    tile = HB * hf + i
                    v.tensor_tensor(rsum[:, tile, :], lg8[:, tile, 0:1], lg8[:, tile, 1:2], ALU.add
                                    ).then_inc(s_route, 1)

            def u_sum(tile):
                u = flat(smx[:, tile % 4])
                dve.wait_ge(s_r_scaled, tile + 1)
                dve.wait_ge(s_down_mm, IC * (tile // HB) + IC)
                v.tensor_tensor(u, banks[4 + tile % HB][:, :], u, ALU.add).then_inc(s_u_ready, 1)
                dve.wait_ge(s_u_ready, tile + 1)
                v.bn_stats(st6[:, tile, :], u).then_inc(s_u_stats_a, 1)
                dve.wait_ge(s_u_stats_a, tile + 1)
                v.bn_aggr(mv[:, tile, :], st6[:, tile, :]).then_inc(s_u_stats_b, 1)

            def ffn_norm(tile):
                u = flat(smx[:, tile % 4])
                dve.wait_ge(s_x2_beta, tile + 1)
                dve.wait_ge(s_u_stats_b, tile + 1)
                v.scalar_tensor_tensor(u, u, mv[:, tile, 0:1], rows[:, 0], ALU.subtract, ALU.mult
                                       ).then_inc(s_u_gamma, 1)
                dve.wait_ge(s_u_rstd, tile + 1)
                dve.wait_ge(s_u_gamma, tile + 1)
                v.scalar_tensor_tensor(acc[:, tile, :], u, stat[:, tile, 1:2], acc[:, tile, :], ALU.mult, ALU.add
                                       ).then_inc(s_w_sum, 1)
                dve.wait_ge(s_w_sum, tile + 1)
                v.bn_stats(st6[:, tile, :], acc[:, tile, :]).then_inc(s_w_stats_a, 1)
                dve.wait_ge(s_w_stats_a, tile + 1)
                v.bn_aggr(mv[:, tile, :], st6[:, tile, :]).then_inc(s_w_stats_b, 1)

            def last_norm(tile):
                dve.wait_ge(s_w_rstd, tile + 1)
                v.tensor_scalar(acc[:, tile, :], acc[:, tile, :], mv[:, tile, 0:1], stat[:, tile, 3:4],
                                ALU.subtract, ALU.mult).then_inc(s_out_ready, 1)

            for tile in range(HB):
                y_stats(tile)
            ffn_lo(1)
            for j in range(2):
                for i in range(2):
                    add_out(units - 2 + j, i, 4 + 2 * j + i, banks[6:8])
                x2(2 * j)
                x2(2 * j + 1)
            ffn_lo(3)
            for tile in range(HB):
                x2_lo(tile)
            ffn_lo(EXPERT)
            for tile in range(HB, B):
                y_stats(tile)
            for c in range(LC):
                product_lo(s_xl_hi, s_xl_lo, 0, c, [qk[0], qk[1]])
            up_lo(0, 0)
            ffn_lo(FC2)
            up_lo(0, 1)
            for c in range(LC):
                product_lo(s_ex_hi, s_ex_lo, 0, c, [wo[0], wo[1]])
            for tile in range(HB, B):
                x2(tile)
            ffn_lo(DOWN[1])
            up_lo(0, 2)
            route(0)
            up_lo(0, 3)
            ffn_lo(DOWN[3])
            for c in range(4, IC):
                up_lo(0, c)
            for tile in range(HB, B):
                x2_lo(tile)
            for tile in range(HB):
                u_sum(tile)
            for c in range(LC):
                product_lo(s_xl_hi, s_xl_lo, 1, c, [qk[0], qk[1]])
            up_lo(1, 0)
            ffn_norm(0)
            up_lo(1, 1)
            for c in range(LC):
                product_lo(s_ex_hi, s_ex_lo, 1, c, [wo[0], wo[1]])
            for c in range(2, IC):
                if c < 5:
                    ffn_norm(c - 1)
                if c >= 4:
                    last_norm(c - 4)
                if c == 2:
                    route(1)
                up_lo(1, c)
            for tile in range(HB, B):
                u_sum(tile)
                ffn_norm(tile)
                if tile > HB:
                    last_norm(tile - 1)
            last_norm(B - 1)

        @block.tensor
        def _(pe):
            mm = nc.tensor.matmul

            def mm3(out, lhs, rhs, first, last):
                mm(out, lhs(0), rhs(1), start=first, stop=False)
                mm(out, lhs(1), rhs(0), start=False, stop=False)
                return mm(out, lhs(0), rhs(0), start=False, stop=last)

            def mm_parts(out, lhs, rhs_both, rhs_hi):
                mm(out, lhs(0), rhs_both, start=True, stop=False)
                return mm(out[:, 1], lhs(1), rhs_hi, start=False, stop=True)

            def dft(hf):
                if hf == 1:
                    pe.wait_ge(s_sq_lo, 4)
                for cc in range(2):
                    pe.wait_ge(s_dft_lo, (2 + 2 * cc) if hf == 0 else (PC_INV + 2 + cc))
                    for j in range(4):
                        for c in (2 * cc, 2 * cc + 1):
                            last = mm3(banks[j][:, :], lambda i: dftC[i][:, c, j * P:(j + 1) * P],
                                       lambda i: dftX(i, hf)[:, c, :], c == 0, c == DC - 1)
                        if cc == 1:
                            last.then_inc(s_dft_mm, 1)

            def corr(tile):
                if tile == 0:
                    pe.wait_ge(s_dft_lo, PC_INV + 1)
                pe.wait_ge(s_sq_lo, 4 * (tile // HB) + 4)
                if tile >= 4:
                    pe.wait_ge(s_top_idx, tile - 3)
                if tile == 4:
                    pe.wait_ge(s_general, 1)
                lt = slice((tile % HB) * P, (tile % HB + 1) * P)
                for j in range(4):
                    last = mm3(banks[4 + tile % 4][:, 0:LAST_LAG], lambda i: sq(i)[:, j, lt],
                               lambda i: dftD[i][:, j, :], j == 0, j == 3)
                last.then_inc(s_corr_mm, 1)

            def count_general(hf):
                pe.wait_ge(s_nonzero, hf + 1)
                out = banks[4 + hf][0:1, 0:1]
                pe.wait_ge(s_top_idx, HB * hf + HB)
                nc.tensor.matmul(out, nonzero[:, hf:hf + 1], ones[:, :], start=True, stop=True).then_inc(s_count_mm, 1)

            pe.wait_ge(s_consts, 5)

            def transposes(tile):
                pe.wait_ge(s_xn_ready, tile + 1)
                if tile >= 2:
                    pe.wait_ge(s_xt_lo, tile - 1)
                out = banks[2 + 2 * (tile % 2)]
                for c in range(DC):
                    last = nc.tensor.transpose(out[:, c * P:(c + 1) * P], rows[:, tile % 2, c * P:(c + 1) * P],
                                               ident[:, :])
                last.then_inc(s_xt_mm, 1)

            dft(0)
            for tile in range(HB):
                corr(tile)
            dft(1)
            count_general(0)
            for tile in range(HB, B):
                corr(tile)
                if tile == HB:
                    pe.wait_ge(s_sq_lo, 8)
                transposes(tile - HB)
            count_general(1)

            def project(which, n, g, j):
                hp, hf = j % 2, j // 2
                if isinstance(g, int):
                    pe.wait_ge(*low_done(piece_qk(g, hp)))
                else:
                    pe.wait_ge(s_w_lo, piece_qk(g, hp) - 2)
                if which == 1 and isinstance(n, int) and n == 0:
                    pe.wait_ge(s_w_lo, CTX_PIECES)
                if which == 0 and isinstance(n, int) and n in (0, 2):
                    pe.wait_ge(s_xt_lo, HB if n == 0 else B)
                src = (xn, cx)[which]
                out = (psQ, psK)[which]
                if due(n):
                    pe.wait_ge((s_q_lo, s_k_lo)[which], n)
                if which == 1 and due(2 * n - 7):
                    pe.wait_ge(s_o_add, 2 * n - 7)
                for c in range(DC):
                    last = mm3(out[:, :], lambda i: wqk[i][:, hp, which, c, :],
                               lambda i: src[i][:, c, hf * HALF:(hf + 1) * HALF], c == 0, c == DC - 1)
                last.then_inc((s_q_mm, s_k_mm)[which], 1)

            def values(m, g, first_tile):
                if isinstance(g, int):
                    pe.wait_ge(*low_done(piece_wv(g)))
                else:
                    pe.wait_ge(s_w_lo, piece_wv(g) - 2)
                if due(m):
                    pe.wait_ge(s_v_lo, m)
                if due(2 * m - 8):
                    pe.wait_ge(s_o_add, 2 * m - 8)
                for i in range(2):
                    tk = slice((first_tile + i) * P, (first_tile + i + 1) * P)
                    for c in range(DC):
                        last = mm3(psV[:, i * 2 * P:(i + 1) * 2 * P], lambda i_: cx[i_][:, c, tk],
                                   lambda i_: wv[i_][:, c, :], c == 0, c == DC - 1)
                last.then_inc(s_v_mm, 1)

            def scores(n):
                pe.wait_ge(s_q_lo, n + 1)
                pe.wait_ge(s_k_lo, n + 1)
                if due(n):
                    pe.wait_ge(s_scores_full, n)
                for b in range(HB):
                    bk = slice(b * P, (b + 1) * P)
                    last = mm_parts(psS[:, b], lambda i: qk[i][:, 0, bk], qk_parts[:, :, 1, bk], qk[0][:, 1, bk])
                last.then_inc(s_scores_mm, 1)

            def turn_probs(n):
                pe.wait_ge(s_probs_ready, n + 1)
                if due(n):
                    pe.wait_ge(s_t_lo, n)
                else:
                    pe.wait_ge(s_xt_lo, B)
                for b in range(HB):
                    last = nc.tensor.transpose(psT[:, b * P:(b + 1) * P], probs[:, b, :], ident[:, :])
                last.then_inc(s_t_mm, 1)

            def attend(n, g, j):
                hp, hf = j % 2, j // 2
                pe.wait_ge(s_t_lo, n + 1)
                if due(4 * g + 2 + 2 * hf):
                    pe.wait_ge(s_v_lo, 4 * g + 2 + 2 * hf)
                if due(n):
                    pe.wait_ge(s_a_lo, n)
                else:
                    pe.wait_ge(s_general, 2)
                for b in range(HB):
                    last = mm_parts(psA[:, b], lambda i: vv[i][:, HB * hf + b, hp * P:(hp + 1) * P],
                                    pt_parts[:, :, b, :], pt[0][:, b, :])
                last.then_inc(s_a_mm, 1)

            def outputs(o, g, first_tile, out=psO):
                hf = first_tile // HB
                if isinstance(g, int):
                    pe.wait_ge(*low_done(piece_wo(g)))
                else:
                    pe.wait_ge(s_w_lo, piece_wo(g) - 2)
                if due(4 * g + 2 + 2 * hf):
                    pe.wait_ge(s_a_lo, 4 * g + 2 + 2 * hf)
                for i in range(2):
                    lt = slice(((first_tile + i) % HB) * P, ((first_tile + i) % HB + 1) * P)
                    if i == 0:
                        pe.wait_ge(s_k_lo, min(o + 4, units) if isinstance(o, int) else o + 4)
                    else:
                        pe.wait_ge(s_v_lo, min(o + 5, units) if isinstance(o, int) else o + 5)
                    if isinstance(o, int) and due(2 * (o - 1) + i + 1):
                        pe.wait_ge(s_o_add, 2 * (o - 1) + i + 1)
                    for hp in range(2):
                        last = mm3(out[i][:, :], lambda i_: at[i_][:, hf, hp, lt], lambda i_: wo[i_][:, hp, :],
                                   hp == 0, hp == 1)
                    last.then_inc(s_o_mm, 1)

            project(1, 0, 0, 0)
            values(0, 0, 0)
            project(0, 0, 0, 0)
            values(1, 0, 2)
            scores(0)
            for tile in range(HB, B):
                transposes(tile)

            def pair_pe(g):
                last = is_last(g)
                for j in range(4):
                    n = 4 * g + j
                    front = not (last and j == 3)
                    if front:
                        project(0, n + 1, *nxt(g, j))
                        project(1, n + 1, *nxt(g, j))
                    turn_probs(n)
                    if not (last and j >= 2):
                        values(n + 2, g + (j >= 2), (2 * j + 4) % B)
                    attend(n, g, j)
                    if front:
                        scores(n + 1)
                    if not (isinstance(g, int) and g == 0 and j < 2):
                        outputs(n - 2, g - (j < 2), (2 * j + 4) % B)

            every_pair(pe, pair_pe)
            for j in range(2):
                pe.wait_ge(s_scores_full, units)
                outputs(units - 2 + j, PAIRS - 1, 4 + 2 * j, banks[6:8])

            def x2_transposes(tile):
                pe.wait_ge(s_x2_ready, tile + 1)
                if due(tile - 1):
                    pe.wait_ge(s_x2_lo, tile - 1)
                if tile == 0:
                    pe.wait_ge(s_t_lo, units)
                    pe.wait_ge(s_v_lo, units)
                    pe.wait_ge(s_o_add, 2 * (units - 2))
                if tile == HB:
                    pe.wait_ge(s_ex_lo, LC)
                    pe.wait_ge(s_route, HB)
                for c in range(DC):
                    last = nc.tensor.transpose(banks[2 + tile % 2][:, c * P:(c + 1) * P],
                                               acc[:, tile, c * P:(c + 1) * P], ident[:, :])
                last.then_inc(s_x2_mm, 1)

            def x_latent(hf):
                pe.wait_ge(*low_done(FFN0 + FC1))
                pe.wait_ge(s_x2_lo, HB * hf + HB)
                for o in range(LC):
                    for c in range(DC):
                        last = mm3(banks[2 + o][:, :], lambda i: wv[i][:, c, tile_cols(o)],
                                   lambda i: xn[i][:, c, half_cols(hf)], c == 0, c == DC - 1)
                    last.then_inc(s_xl_mm, 1)

            def up(hf, o):
                n = IC * hf + o
                if n == 0:
                    pe.wait_ge(s_q_lo, units)
                    pe.wait_ge(s_k_lo, units)
                    for k in UP:
                        pe.wait_ge(*low_done(FFN0 + k))
                if due(n - 1):
                    pe.wait_ge(s_up_lo, n - 1)
                if due(HB * hf):
                    pe.wait_ge(s_r_scaled, HB * hf)
                for c in range(DC):
                    last = mm3(banks[o % 2][:, :], lambda i: cx[i][:, c, tile_cols(o)],
                               lambda i: xn[i][:, c, half_cols(hf)], c == 0, c == DC - 1)
                last.then_inc(s_up_mm, 1)

            def expert_out(hf):
                pe.wait_ge(*low_done(FFN0 + EXPERT))
                pe.wait_ge(s_xl_lo, LC * (hf + 1))
                for o in range(LC):
                    for c in range(LC):
                        last = mm3(banks[2 + o][:, :], lambda i: expert[i][:, c, tile_cols(o)],
                                   lambda i: qk[i][:, c, :], c == 0, c == LC - 1)
                    last.then_inc(s_ex_mm, 1)

            def logits(hf):
                pe.wait_ge(s_gate_lo, 1)
                pe.wait_ge(s_ex_lo, LC * (hf + 1))
                for b in range(HB):
                    for c in range(DC):
                        last = mm3(banks[2][:, b * NE:(b + 1) * NE],
                                   lambda i: xn[i][:, c, tile_cols(HB * hf + b)], lambda i: gate[i][:, c, :],
                                   c == 0, c == DC - 1)
                last.then_inc(s_lg_mm, 1)

            def down(hf, c):
                n = IC * hf + c
                if hf == 0 and c % 2 == 0:
                    pe.wait_ge(*low_done(FFN0 + DOWN[c // 2]))
                pe.wait_ge(s_up_lo, n + 1)
                if c == 0:
                    if due(HB * hf):
                        pe.wait_ge(s_u_ready, HB * hf)
                    if hf == 0:
                        pe.wait_ge(s_a_lo, units)
                        pe.wait_ge(s_o_add, 2 * units)
                for b in range(HB):
                    last = mm3(banks[4 + b][:, :], lambda i: hidden(i, c)[:, tile_cols(b)],
                               lambda i: wdown[i][c // 4][:, c % 4, :], c == 0, c == IC - 1)
                last.then_inc(s_down_mm, 1)

            def routed(hf, b):
                tile = HB * hf + b
                if b == 0:
                    pe.wait_ge(*low_done(FFN0 + FC2))
                pe.wait_ge(s_up_lo, IC * (hf + 1))
                if due(tile - 1):
                    pe.wait_ge(s_r_scaled, tile - 1)
                for c in range(LC):
                    last = mm3(banks[tile % 2][:, :], lambda i: wo[i][:, c, tile_cols(b)],
                               lambda i: ext[i][:, c, :], c == 0, c == LC - 1)
                last.then_inc(s_r_mm, 1)

            for tile in range(HB):
                x2_transposes(tile)
            for hf in range(2):
                x_latent(hf)
                up(hf, 0)
                up(hf, 1)
                expert_out(hf)
                for c in range(IC):
                    down(hf, c)
                    if c + 2 < IC:
                        up(hf, c + 2)
                    if c == 0:
                        logits(hf)
                if hf == 0:
                    for tile in range(HB, B):
                        x2_transposes(tile)
                for b in range(HB):
                    routed(hf, b)


def layouts(i):
    x = np.asarray(i["x"])
    n = np.arange(D)
    f = np.arange(D // 2)
    ang = 2 * np.pi * np.outer(n, f) / D
    fwd = np.concatenate([np.cos(ang), np.sin(ang)], axis=1)
    fwd[:, D // 2] = np.cos(np.pi * n)
    lag = np.arange(1, LAST_LAG + 1)
    wave = np.cos(2 * np.pi * np.outer(f, lag) / D)
    inv = np.concatenate([wave, wave], axis=0) * 2 / D
    inv[0] /= 2
    inv[D // 2] = np.cos(np.pi * lag) / D
    chunks = lambda m: m.reshape(DC, P, -1).transpose(1, 0, 2)
    two = lambda m: [m[:, 0:2].reshape(P, PIECE), m[:, 2:4].reshape(P, PIECE)]
    C, Dm = chunks(fwd.astype(np.float32)), chunks(inv.astype(np.float32))
    xT = chunks(np.ascontiguousarray(x.reshape(TOK, D).T))
    c0, c1 = two(C)
    a0, a1 = two(xT[:, :, :HALF])
    b0, b1 = two(xT[:, :, HALF:])
    ctxT = np.asarray(i["ctx_4096"]).reshape(TOK, D).T.reshape(DC, P, TOK)
    xf = x.reshape(TOK, D)
    by_chunk = lambda w: np.asarray(w).reshape(-1, P, w.shape[1]).transpose(1, 0, 2).reshape(P, -1)
    up = np.asarray(i["L0_ffn_up_w"])
    down = np.asarray(i["L0_ffn_down_w"]).reshape(4, 2, P, D).transpose(0, 2, 1, 3).reshape(4, P, PIECE)
    fc1, fc2 = by_chunk(i["L0_ffn_fc1_w"]), by_chunk(i["L0_ffn_fc2_w"])
    gx = np.concatenate([by_chunk(i["L0_ffn_expert_w"]), by_chunk(i["L0_ffn_gate_w"])], axis=1)
    heads = lambda w: np.asarray(w).reshape(H, P, DC, P).transpose(0, 3, 2, 1)
    return {
        "dft": np.stack([c0, a0, c1, a1, Dm.reshape(P, PIECE), b0, b1]),
        "x": xf,
        "xx": np.concatenate([xf, xf], axis=1).reshape(-1, 1),
        "ln_w": np.asarray(i["L0_xattn_ln_weight"]),
        "mask": np.asarray(i["mask_BxSxS2_bk0"]),
        "ctxT": ctxT,
        "wqk": np.stack([heads(i["L0_xattn_w_q"]), heads(i["L0_xattn_w_k"])], axis=2).reshape(H, P, PIECE),
        "wv": np.asarray(i["L0_xattn_w_v"]).reshape(PAIRS, 2 * P, DC, P).transpose(0, 3, 2, 1).reshape(PAIRS, P, PIECE),
        "wo": np.asarray(i["L0_xattn_w_out"]).reshape(D, PAIRS, 2, P).transpose(1, 3, 2, 0).reshape(PAIRS, P, PIECE),
        "bias": np.asarray(i["L0_xattn_position_bias"]),
        "ffn": np.stack([*up.reshape(DC, P, PIECE), fc1, fc2, *down]),
        "gx": gx,
        "gamma": np.asarray(i["L0_ffn_ln_gamma"]),
        "beta": np.asarray(i["L0_ffn_ln_beta"]),
    }


def kernel(**inputs):
    import concourse.bacc as bacc
    from concourse.bass_utils import run_bass_kernel_spmd as run

    nc = bacc.Bacc("TRN2", target_bir_lowering=False, num_devices=1)
    arrays, t = {}, {}
    for name, a in layouts(inputs).items():
        arrays["in_" + name] = np.ascontiguousarray(a)
        t[name] = nc.dram_tensor("in_" + name, a.shape, mybir.dt.from_np(a.dtype), kind="ExternalInput").ap()
    t["out"] = nc.dram_tensor("out", (TOK, D), F32, kind="ExternalOutput").ap()
    build(nc, t)
    r = run(nc, [arrays], core_ids=[0])
    return r.results[0]["out"].reshape(B, P, D)
```

```python
from contextlib import ExitStack

import concourse.bass as bass
from concourse import mybir
import numpy as np

F32 = mybir.dt.float32
F32R = mybir.dt.float32r
U32 = mybir.dt.uint32
U8 = mybir.dt.uint8
ALU = mybir.AluOpType
ACT = mybir.ActivationFunctionType
AX = mybir.AxisListType

P = 128
B = 8
D = 512
DC = D // P
TOK = B * P
HALF = TOK // 2
HB = B // 2
H = 32
PAIRS = H // 2
INT = 1024
IC = INT // P
LAT = 256
LC = LAT // P
NE = 8
LAGS = 6
EPS = 1e-5
FAR = 2.0 ** 100
PIECE = 1024
SLOTS = 4
WARM_UPS = 48
RING = 4

DFT_PIECES = 7
LAST_LAG = D // 2
CTX_PIECES = DC
FFN_PIECES = 11

PC_WV0, PC_QK00, PC_QK01 = CTX_PIECES, CTX_PIECES + 1, CTX_PIECES + 2
LOOP0 = CTX_PIECES + 3


def build(nc, t):
    units = 4 * PAIRS
    with ExitStack() as ctx:
        def sb(name, shape, dt=F32):
            return ctx.enter_context(nc.sbuf_tensor(name, shape, dt))

        def sem(name):
            return ctx.enter_context(nc.semaphore(name))

        def hilo(name, shape):
            return sb(name + "_hi", shape, F32R), sb(name + "_lo", shape, F32R)

        xn = hilo("xn", [P, DC, TOK])
        cx = hilo("cx", [P, DC, TOK])
        acc = sb("acc", [P, B, D])
        wqk = hilo("wqk", [P, 2, 2, DC, P])
        wv = hilo("wv", [P, DC, 2 * P])
        wo = hilo("wo", [P, 2, D])
        vv = hilo("vv", [P, B, 2 * P])
        at = hilo("at", [P, 2, 2, HALF])
        qk_parts = sb("qk", [P, 2, 2, HALF], F32R)
        pt_parts = sb("pt", [P, 2, HB, P], F32R)
        qk = [qk_parts[:, i] for i in (0, 1)]
        pt = [pt_parts[:, i] for i in (0, 1)]
        rest = sb("rest", [P, HB, P])
        ext = hilo("ext", [P, 2, D])
        smx = sb("smx", [P, 4, HB, P])
        raw = sb("raw", [P, SLOTS, PIECE])
        far = sb("far", [P, B, P])
        bias = sb("bias", [P, 2, P])
        ident = sb("ident", [P, P])
        rows = sb("rows", [P, 2, D])
        lnw = sb("lnw", [P, D])
        m8 = sb("m8", [P, B, P], U8)
        scores_sb, exps, probs, bm = (smx[:, i] for i in range(4))

        gate = hilo("gate", [P, DC, NE])
        lg8 = sb("lg8", [P, B, 8])
        rsum = sb("rsum", [P, B, 1])
        half_pow = sb("half_pow", [P, 1])
        rowbase = sb("rowbase", [P, 1])
        topv = sb("topv", [P, B, 16])
        topi = sb("topi", [P, B, 8], U32)
        gidx = sb("gidx", [P, B, 8], U32)
        topm = sb("topm", [P, B, 3])
        ones = sb("ones", [P, 1])
        others = sb("others", [P, 2])
        nonzero = sb("nonzero", [P, 2])
        general = sb("general", [P, 2], mybir.dt.int32)
        wts = sb("wts", [P, B, 8])
        wsum = sb("wsum", [P, B, 2])
        st6 = sb("st6", [P, B, 6])
        mv = sb("mv", [P, B, 2])
        stat = sb("stat", [P, B, 6])
        prep = sb("prep", [P, 7, B])
        nmax = sb("nmax", [P, 2, HB])
        esum = sb("esum", [P, 3, HB])

        psum = ctx.enter_context(nc.psum_tensor("psum", [P, 8, 512], F32))
        banks = [psum[:, i] for i in range(8)]
        psQ, psK, psT, psV = banks[0:4]
        psO = [psK, psV]

        def parts(first):
            return psum[:, first:first + 2].rearrange("p k (b i n) -> p (k b) i n", b=2, i=2)

        psA, psS = parts(4), parts(6)
        LATE = {4 * PAIRS - 3: (banks[0], banks[6]), 4 * PAIRS - 2: (banks[7], banks[1]),
                4 * PAIRS - 1: (banks[0], banks[6])}

        def out_banks(o):
            return LATE.get(o, psO) if isinstance(o, int) else psO

        s_dft_hi = sem("dft_hi")
        s_dft_lo = sem("dft_lo")
        s_w_hi = sem("w_hi")
        s_w_lo = sem("w_lo")
        s_consts = sem("consts")
        s_x_landed = sem("x_landed")
        s_mask_landed = sem("mask_landed")
        s_lnw_landed = sem("lnw_landed")
        s_far_ready = sem("far_ready")
        s_dft_mm = sem("dft_mm")
        s_sq_done = sem("sq_done")
        s_sq_hi = sem("sq_hi")
        s_sq_lo = sem("sq_lo")
        s_corr_mm = sem("corr_mm")
        s_top_val = sem("top_val")
        s_top_idx = sem("top_idx")
        s_gather_idx = sem("gather_idx")
        s_top_max = sem("top_max")
        s_w_exp = sem("w_exp")
        s_w_rec = sem("w_rec")
        s_w_ready = sem("w_ready")
        s_w0_ready = sem("w0_ready")
        s_acc_scaled = sem("acc_scaled")
        s_acc_sum = [sem(f"acc_sum{i}") for i in range(2)]
        s_stats_a = sem("stats_a")
        s_stats_b = sem("stats_b")
        s_var_eps = sem("var_eps")
        s_rstd = sem("rstd")
        s_row_normed = sem("row_normed")
        s_mirrored = sem("mirrored")
        s_lag0 = sem("lag0")
        s_others = sem("others")
        s_nonzero = sem("nonzero")
        s_count_mm = sem("count_mm")
        s_general = sem("general")
        s_prep = sem("prep")
        s_xn_ready = sem("xn_ready")
        s_acc_x1 = sem("acc_x1")
        s_xt_mm = sem("xt_mm")
        s_xt_hi = sem("xt_hi")
        s_xt_lo = sem("xt_lo")
        s_q_mm = sem("q_mm")
        s_q_hi = sem("q_hi")
        s_q_lo = sem("q_lo")
        s_k_mm = sem("k_mm")
        s_k_hi = sem("k_hi")
        s_k_lo = sem("k_lo")
        s_t_mm = sem("t_mm")
        s_t_hi = sem("t_hi")
        s_t_lo = sem("t_lo")
        s_v_mm = sem("v_mm")
        s_v_hi = sem("v_hi")
        s_v_lo = sem("v_lo")
        s_a_mm = sem("a_mm")
        s_a_hi = sem("a_hi")
        s_a_rest = sem("a_rest")
        s_a_lo = sem("a_lo")
        s_scores_mm = sem("scores_mm")
        s_scores_sum = sem("scores_sum")
        s_scores_full = sem("scores_full")
        s_scores_max = sem("scores_max")
        s_max_neg = sem("max_neg")
        s_exp_done = sem("exp_done")
        s_sum_clamped = sem("sum_clamped")
        s_sum_inverse = sem("sum_inverse")
        s_probs_ready = sem("probs_ready")
        s_bm_ready = sem("bm_ready")
        s_o_mm = sem("o_mm")
        s_o_add = sem("o_add")
        s_stored = sem("stored")
        s_f_lo = sem("f_lo")
        s_gate_hi = sem("gate_hi")
        s_gate_lo = sem("gate_lo")
        s_rows_landed = sem("rows_landed")
        s_y_stats_a = sem("y_stats_a")
        s_y_stats_b = sem("y_stats_b")
        s_y_eps = sem("y_eps")
        s_y_rstd = sem("y_rstd")
        s_x2_ready = sem("x2_ready")
        s_x2_mm = sem("x2_mm")
        s_x2_hi = sem("x2_hi")
        s_x2_lo = sem("x2_lo")
        s_x2_beta = sem("x2_beta")
        s_xl_mm = sem("xl_mm")
        s_xl_hi = sem("xl_hi")
        s_xl_lo = sem("xl_lo")
        s_ex_mm = sem("ex_mm")
        s_ex_hi = sem("ex_hi")
        s_ex_lo = sem("ex_lo")
        s_lg_mm = sem("lg_mm")
        s_lg_copied = sem("lg_copied")
        s_lg_turned = sem("lg_turned")
        s_lg_top = sem("lg_top")
        s_route = sem("route")
        s_up_mm = sem("up_mm")
        s_up_relu = sem("up_relu")
        s_up_sq = sem("up_sq")
        s_up_hi = sem("up_hi")
        s_up_lo = sem("up_lo")
        s_down_mm = sem("down_mm")
        s_r_mm = sem("r_mm")
        s_r_scaled = sem("r_scaled")
        s_u_ready = sem("u_ready")
        s_u_stats_a = sem("u_stats_a")
        s_u_stats_b = sem("u_stats_b")
        s_u_eps = sem("u_eps")
        s_u_rstd = sem("u_rstd")
        s_u_gamma = sem("u_gamma")
        s_w_sum = sem("w_sum")
        s_w_stats_a = sem("w_stats_a")
        s_w_stats_b = sem("w_stats_b")
        s_w_eps = sem("w_eps")
        s_w_rstd = sem("w_rstd")
        s_w_neg = sem("w_neg")
        s_w_shift = sem("w_shift")
        s_out_ready = sem("out_ready")
        s_landed = [sem(f"landed{i}") for i in range(SLOTS)]
        s_got = [[sem(f"got{hf}_{i}") for i in range(RING)] for hf in range(2)]
        s_bias_landed = [sem(f"bias_landed{i}") for i in range(2)]

        def due(count):
            return not isinstance(count, int) or count > 0

        block = ctx.enter_context(nc.Block())

        def flat(x):
            n = len(x.shape)
            return x if n == 2 else x.rearrange({3: "p a b -> p (a b)", 4: "p a b c -> p (a b c)",
                                                 5: "p a b c d -> p (a b c d)"}[n])

        dftC = [at[i].rearrange("p a b n -> p (a b) n") for i in (0, 1)]
        def dftX(i, hf):
            x = wqk[i].rearrange("p a b c n -> p (a b c n)") if hf == 0 else vv[i].rearrange("p b n -> p (b n)")
            return x.rearrange("p (c n) -> p c n", c=DC)
        dftD = [ext[i].rearrange("p a n -> p (a n)").rearrange("p (c n) -> p c n", c=DC) for i in (0, 1)]

        def sq(i):
            return xn[i][:, :, HALF:TOK]

        PC_INV = 4

        def dft_dst(i, piece):
            return (dftC[i][:, 0:2], dftX(i, 0)[:, 0:2], dftC[i][:, 2:4], dftX(i, 0)[:, 2:4], ext[i][:, :, :],
                    dftX(i, 1)[:, 0:2], dftX(i, 1)[:, 2:4])[piece]

        def shifted(hf, n):
            return flat(rest) if hf == 1 and n % RING == RING - 1 else flat(smx[:, n % RING])

        def slot_at(w):
            return (DFT_PIECES + w) % SLOTS

        def landed_count(w):
            return 16 * ((DFT_PIECES + w) // SLOTS + 1)

        def raw2(slot):
            return raw[:, slot].rearrange("p (a n) -> p a n", a=2)

        def turned(tile):
            return banks[2 - 2 * (tile % 2)].rearrange("p (c n) -> p c n", c=DC)

        def piece_qk(g, hp):
            if isinstance(g, int) and g == 0:
                return (PC_QK00, PC_QK01)[hp]
            return LOOP0 + 4 * (g - 1) + (0, 3)[hp]

        def piece_wv(g):
            if isinstance(g, int) and g == 0:
                return PC_WV0
            return LOOP0 + 4 * (g - 1) + 1

        def piece_wo(g):
            if isinstance(g, int) and g == PAIRS - 1:
                return LOOP0 + 4 * g
            return LOOP0 + 4 * g + 2

        def slot_of(w0, k):
            return (DFT_PIECES + LOOP0 + k) % SLOTS

        def rounds(g, k):
            return g + (DFT_PIECES + LOOP0 + k) // SLOTS + 1

        def nxt(g, j):
            return (g, j + 1) if j < 3 else (g + 1, 0)

        def every_pair(engine, body):
            body(0)
            with engine.Fori(1, PAIRS - 1) as g:
                body(g)
            body(PAIRS - 1)

        def heads_out(i, j):
            return at[i][:, j // 2, j % 2].rearrange("p (b n) -> p b n", b=HB)

        def is_first(g):
            return isinstance(g, int) and g == 0

        def is_last(g):
            return isinstance(g, int) and g == PAIRS - 1

        FFN0 = LOOP0 + 4 * (PAIRS - 1) + 1
        UP, FC1, EXPERT, FC2, DOWN = (0, 1, 2, 3), 4, 5, 6, (7, 8, 9, 10)
        BY_VECTOR = (3, 5, 6, 8, 10)
        expert = [flat(pt[i]).rearrange("p (c n) -> p c n", c=LC) for i in (0, 1)]
        wdown = [[flat(wqk[i]).rearrange("p (c n) -> p c n", c=4), flat(vv[i]).rearrange("p (c n) -> p c n", c=4)]
                 for i in (0, 1)]
        GX = LC * LAT + DC * NE

        def ffn_dst(i, k):
            if k in UP:
                return cx[i][:, k]
            if k == FC1:
                return flat(wv[i])
            if k == EXPERT:
                return flat(pt[i])
            if k == FC2:
                return flat(ext[i])
            d = k - DOWN[0]
            return flat(wdown[i][d // 2][:, 2 * (d % 2):2 * (d % 2) + 2, :])

        def ffn_src(k):
            return raw[:, (DFT_PIECES + FFN0 + k) % SLOTS, 0:LC * LAT if k == EXPERT else PIECE]

        def low_done(k):
            if k < 0:
                return s_dft_lo, k + DFT_PIECES + 1
            if k < FFN0:
                return s_w_lo, k + 1
            f = k - FFN0
            if f in BY_VECTOR:
                return s_f_lo, BY_VECTOR.index(f) + 1
            return s_w_lo, k + 1 - len([b for b in BY_VECTOR if b < f])

        def hidden(i, c):
            return at[i][:, (c % 4) // 2, c % 2]

        def tile_cols(tile):
            return slice(tile * P, (tile + 1) * P)

        def half_cols(hf):
            return slice(hf * HALF, (hf + 1) * HALF)

        @block.sync
        def _(sp):
            def stage(piece, src):
                old = piece - SLOTS - DFT_PIECES
                if isinstance(old, int):
                    if old + DFT_PIECES >= 0:
                        sp.wait_ge(*low_done(old))
                    if old == FFN0 + EXPERT:
                        sp.wait_ge(s_gate_lo, 1)
                else:
                    sp.wait_ge(s_w_lo, old + 1)
                return src

            def load(piece, slot, src):
                stage(piece, src)
                sp.dma_start(raw[:, slot, 0:src.shape[1]], src).then_inc(s_landed[slot], 16)

            def load_rows(hf):
                sp.dma_start(acc[:, HB * hf:HB * hf + HB, :],
                             t["x"].rearrange("(b p) d -> p b d", p=P)[:, HB * hf:HB * hf + HB, :]
                             ).then_inc(s_x_landed, 16)

            for p in range(DFT_PIECES):
                if p == PC_INV:
                    load_rows(0)
                load(p, p % SLOTS, t["dft"][p])
            sp.dma_start(m8[:, :, :], t["mask"].rearrange("b q k -> q b k")).then_inc(s_mask_landed, 16)
            for c in range(CTX_PIECES):
                load(DFT_PIECES + c, slot_at(c), t["ctxT"][c])
                if c == 0:
                    sp.dma_start(lnw[:, :], t["ln_w"].partition_broadcast(P)).then_inc(s_lnw_landed, 16)
                    load_rows(1)

            def load_bias(g, hp):
                if due(4 * g - 1 + hp):
                    sp.wait_ge(s_bm_ready, 4 * g - 1 + hp)
                sp.dma_start(bias[:, hp, :], row(t["bias"], 2 * g + hp)).then_inc(s_bias_landed[hp], 16)

            def row(x, i):
                return x[i] if isinstance(i, int) else x[bass.ds(i, 1)].rearrange("o p n -> (o p) n")

            load(DFT_PIECES + PC_WV0, slot_at(PC_WV0), t["wv"][0])
            for hp in range(2):
                load_bias(0, hp)
                pc = DFT_PIECES + (PC_QK00, PC_QK01)[hp]
                load(pc, pc % SLOTS, t["wqk"][hp])

            def pair_loads(g):
                base = DFT_PIECES + LOOP0 + 4 * g
                if is_last(g):
                    load(base, slot_of(g, 0), row(t["wo"], g))
                    return
                load(base, slot_of(g, 0), row(t["wqk"], 2 * g + 2))
                load(base + 1, slot_of(g, 1), row(t["wv"], g + 1))
                load(base + 2, slot_of(g, 2), row(t["wo"], g))
                load_bias(g + 1, 0)
                load(base + 3, slot_of(g, 3), row(t["wqk"], 2 * g + 3))
                load_bias(g + 1, 1)

            every_pair(sp, pair_loads)

            sp.wait_ge(s_xt_mm, B)
            sp.dma_start(rows[:, 0], t["gamma"].partition_broadcast(P)).then_inc(s_rows_landed, 16)
            sp.dma_start(rows[:, 1], t["beta"].partition_broadcast(P)).then_inc(s_rows_landed, 16)
            for k in range(FFN_PIECES):
                pc = DFT_PIECES + FFN0 + k
                load(pc, pc % SLOTS, t["gx"] if k == EXPERT else t["ffn"][k - (k > EXPERT)])
            for tile in range(B):
                sp.wait_ge(s_out_ready, tile + 1)
                sp.dma_start(t["out"][tile_cols(tile), :], acc[:, tile, :]).then_inc(s_stored, 16)
            sp.wait_ge(s_stored, 16 * B)

        @block.gpsimd
        def _(pool):
            g = nc.gpsimd
            g.memset(half_pow[:, :], -0.5).then_inc(s_consts, 1)
            g.iota(rowbase[:, :], [[0, 1]], base=1, channel_multiplier=2 * D,
                   allow_small_or_imprecise_dtypes=True).then_inc(s_consts, 1)
            g.memset(ident[:, :], 0.0).then_inc(s_consts, 1)
            pool.wait_ge(s_consts, 3)
            g.affine_select(out=ident[:, :], in_=ident[:, :], compare_op=ALU.not_equal, fill=1.0, base=0,
                            pattern=[[-1, P]], channel_multiplier=1).then_inc(s_consts, 1)
            g.memset(ones[:, :], 1.0).then_inc(s_consts, 1)

            def split_lo(w, src, dst_hi, dst_lo):
                pool.wait_ge(s_w_hi, w + 1)
                g.tensor_tensor(dst_lo, src, dst_hi, ALU.subtract).then_inc(s_w_lo, 1)

            def shifted_rows(hf):
                pool.wait_ge(s_general, hf + 1)
                count = pool.value_load(general[0:1, hf:hf + 1], min_val=0, max_val=1)
                with pool.If(count != 0):
                    for n in range(HB * (LAGS - 1)):
                        tile, k = HB * hf + n // (LAGS - 1), n % (LAGS - 1)
                        if n >= RING:
                            pool.wait_ge(s_acc_sum[hf], n - RING + 1)
                        g.indirect_dma_start(shifted(hf, n), None, t["xx"],
                                             bass.IndirectOffsetOnAxis(ap=gidx[:, tile, k:k + 1], axis=0)
                                             ).then_inc(s_got[hf][n % RING], 16)
                    pool.wait_ge(s_acc_sum[hf], HB * (LAGS - 1))

            def weighted_row(tile):
                pool.wait_ge(s_row_normed, tile + 1)
                if tile == 0:
                    pool.wait_ge(s_lnw_landed, 16)
                g.tensor_tensor(rows[:, tile % 2], rows[:, tile % 2], lnw[:, :], ALU.mult).then_inc(s_xn_ready, 1)

            def factors(hf):
                pool.wait_ge(s_stats_b, HB * hf + HB)
                cols, n0 = slice(HB * hf, HB * hf + HB), 5 * hf
                mean, var = mv[:, cols, 0], mv[:, cols, 1]
                g.tensor_scalar(prep[:, 0, cols], var, EPS, 0.25, ALU.add, ALU.mult).then_inc(s_prep, 1)
                g.tensor_scalar(prep[:, 1, cols], var, 1 + EPS, EPS * EPS, ALU.mult, ALU.add).then_inc(s_prep, 1)
                g.tensor_scalar(prep[:, 6, cols], mean, -1.0, None, ALU.mult).then_inc(s_prep, 1)
                pool.wait_ge(s_prep, n0 + 3)
                g.tensor_tensor(prep[:, 2:4, cols], prep[:, 0:2, cols],
                                half_pow[:, :].unsqueeze(2).to_broadcast([P, 2, HB]), ALU.pow).then_inc(s_prep, 1)
                pool.wait_ge(s_prep, n0 + 4)
                g.tensor_tensor(prep[:, 4:6, cols], prep[:, 2:4, cols],
                                prep[:, 6:7, cols].to_broadcast([P, 2, HB]), ALU.mult).then_inc(s_prep, 1)

            def bias_and_mask(n, g, j):
                hp, hf = j % 2, j // 2
                pool.wait_ge(s_bias_landed[hp], 16 * (g + 1))
                if due(n):
                    pool.wait_ge(s_scores_sum, n)
                if isinstance(n, int) and n == 0:
                    pool.wait_ge(s_far_ready, 1)
                g_ = bias[:, hp:hp + 1, :].to_broadcast([P, HB, P])
                nc.gpsimd.tensor_tensor(bm, far[:, HB * hf:HB * hf + HB, :], g_, ALU.add).then_inc(s_bm_ready, 1)

            wflat = [(flat(wv[0]), flat(wv[1])), (flat(wqk[0][:, 0]), flat(wqk[1][:, 0])),
                     (flat(wqk[0][:, 1]), flat(wqk[1][:, 1])), (flat(wo[0]), flat(wo[1]))]
            WV, WQ0, WQ1, WO = range(4)

            for c in range(CTX_PIECES):
                split_lo(c, raw[:, slot_at(c)], cx[0][:, c], cx[1][:, c])
            split_lo(PC_WV0, raw[:, slot_at(PC_WV0)], *wflat[WV])
            split_lo(PC_QK00, raw[:, slot_at(PC_QK00)], *wflat[WQ0])
            shifted_rows(0)
            factors(0)
            weighted_row(0)
            weighted_row(1)
            split_lo(PC_QK01, raw[:, slot_at(PC_QK01)], *wflat[WQ1])
            weighted_row(2)
            weighted_row(3)
            bias_and_mask(0, 0, 0)
            shifted_rows(1)
            bias_and_mask(1, 0, 1)
            factors(1)
            for tile in range(HB, B):
                weighted_row(tile)

            def pair_pool(g):
                last = is_last(g)
                for j in range(4):
                    n = 4 * g + j
                    if not (last and j == 3 or is_first(g) and j == 0):
                        bias_and_mask(n + 1, *nxt(g, j))
                    if j == 1 and not last:
                        split_lo(piece_qk(g + 1, 0), raw[:, slot_of(g, 0)], *wflat[WQ0])
                        split_lo(piece_wv(g + 1), raw[:, slot_of(g, 1)], *wflat[WV])
                    if j == 2:
                        split_lo(piece_wo(g), raw[:, slot_of(g, 0 if last else 2)], *wflat[WO])
                        if not last:
                            split_lo(piece_qk(g + 1, 1), raw[:, slot_of(g, 3)], *wflat[WQ1])

            every_pair(pool, pair_pool)

            def power(s_eps, s_out, var, mid, dst, tile):
                g = nc.gpsimd
                g.tensor_scalar(mid, var, EPS, None, ALU.add).then_inc(s_eps, 1)
                pool.wait_ge(s_eps, tile + 1)
                g.tensor_tensor(dst, mid, half_pow[:, :], ALU.pow).then_inc(s_out, 1)

            def ffn_lo(k):
                if k not in BY_VECTOR:
                    split_low(k)

            def split_low(k):
                pool.wait_ge(s_w_hi, FFN0 + k + 1)
                nc.gpsimd.tensor_tensor(ffn_dst(1, k), ffn_src(k), ffn_dst(0, k), ALU.subtract
                                        ).then_inc(s_w_lo, 1)

            def y_power(tile):
                pool.wait_ge(s_y_stats_b, tile + 1)
                power(s_y_eps, s_y_rstd, mv[:, tile, 1:2], stat[:, tile, 0:1], stat[:, tile, 1:2], tile)

            def add_beta(tile):
                pool.wait_ge(s_x2_mm, tile + 1)
                if tile == 0:
                    pool.wait_ge(s_rows_landed, 32)
                nc.gpsimd.tensor_tensor(acc[:, tile, :], acc[:, tile, :], rows[:, 1], ALU.add
                                        ).then_inc(s_x2_beta, 1)

            def u_power(tile):
                pool.wait_ge(s_u_stats_b, tile + 1)
                power(s_u_eps, s_u_rstd, mv[:, tile, 1:2], stat[:, tile, 0:1], stat[:, tile, 1:2], tile)

            def w_power(tile):
                pool.wait_ge(s_w_stats_b, tile + 1)
                nc.gpsimd.tensor_scalar(stat[:, tile, 4:5], mv[:, tile, 0:1], -1.0, None, ALU.mult
                                        ).then_inc(s_w_neg, 1)
                power(s_w_eps, s_w_rstd, mv[:, tile, 1:2], stat[:, tile, 2:3], stat[:, tile, 3:4], tile)
                pool.wait_ge(s_w_neg, tile + 1)
                pool.wait_ge(s_w_rstd, tile + 1)
                nc.gpsimd.tensor_tensor(stat[:, tile, 5:6], stat[:, tile, 4:5], stat[:, tile, 3:4], ALU.mult
                                        ).then_inc(s_w_shift, 1)

            for k in UP[:3]:
                ffn_lo(k)
            for tile in range(HB):
                y_power(tile)
            ffn_lo(FC1)
            ffn_lo(DOWN[0])
            for tile in range(HB, B):
                y_power(tile)
            ffn_lo(DOWN[2])
            for tile in range(B):
                add_beta(tile)
            for tile in range(HB):
                u_power(tile)
            for tile in range(HB):
                w_power(tile)
            for tile in range(HB, B):
                u_power(tile)
                if tile > HB:
                    w_power(tile - 1)
            w_power(B - 1)

        @block.scalar
        def _(act):
            a = nc.scalar

            def copy_hi(dst, src):
                return a.activation(dst, src, ACT.Copy)

            def dft_hi(p):
                act.wait_ge(s_landed[p % SLOTS], 16 * (p // SLOTS + 1))
                copy_hi(dft_dst(0, p), raw2(p % SLOTS)).then_inc(s_dft_hi, 1)

            def square(hf, j):
                n = 4 * hf + j
                act.wait_ge(s_dft_mm, n + 1)
                a.activation(banks[j][:, :], banks[j][:, :], ACT.Square).then_inc(s_sq_done, 1)
                act.wait_ge(s_sq_done, n + 1)
                if j == 0 and hf == 1:
                    act.wait_ge(s_corr_mm, HB)
                copy_hi(sq(0)[:, j], banks[j][:, :]).then_inc(s_sq_hi, 1)

            def lag0(tile):
                if tile % HB == 0:
                    act.wait_ge(s_x_landed, 16 * (tile // HB + 1))
                if due(tile):
                    act.wait_ge(s_lag0, tile)
                a.activation(flat(rest), acc[:, tile, :], ACT.Square, accum_out=topv[:, tile, 0:1]
                             ).then_inc(s_lag0, 1)

            def mirror(tile):
                bank = banks[4 + tile % 4]
                act.wait_ge(s_corr_mm, tile + 1)
                a.activation(bank[:, LAST_LAG:D - 1], bank[:, 0:LAST_LAG - 1][:, ::-1], ACT.Copy
                             ).then_inc(s_mirrored, 1)

            def weigh(tile):
                act.wait_ge(s_top_max, 2 * tile + 2)
                a.activation(wts[:, tile, 0:LAGS], topv[:, tile, 0:LAGS], ACT.Exp, bias=topm[:, tile, 1:2],
                             accum_out=wsum[:, tile, 0:1]).then_inc(s_w_exp, 1)

            def scale_rows(tile):
                act.wait_ge(s_w0_ready, tile + 1)
                a.activation(acc[:, tile, :], acc[:, tile, :], ACT.Copy, scale=wsum[:, tile, 1:2]
                             ).then_inc(s_acc_scaled, 1)

            def normed_row(tile):
                if tile % HB == 0:
                    act.wait_ge(s_prep, 5 * (tile // HB) + 5)
                if due(tile - 1):
                    act.wait_ge(s_xt_mm, tile - 1)
                a.activation(rows[:, tile % 2], acc[:, tile, :], ACT.Identity, bias=prep[:, 5, tile:tile + 1],
                             scale=prep[:, 3, tile:tile + 1]).then_inc(s_row_normed, 1)

            def double(tile):
                a.activation(acc[:, tile, :], acc[:, tile, :], ACT.Identity, bias=prep[:, 4, tile:tile + 1],
                             scale=prep[:, 2, tile:tile + 1]).then_inc(s_acc_x1, 1)

            def xt_hi(tile):
                act.wait_ge(s_xt_mm, tile + 1)
                if tile == HB:
                    act.wait_ge(s_corr_mm, B)
                copy_hi(xn[0][:, :, tile * P:(tile + 1) * P], turned(tile)).then_inc(s_xt_hi, 1)

            def ctx_hi(c):
                act.wait_ge(s_landed[slot_at(c)], landed_count(c))
                copy_hi(cx[0][:, c], raw[:, slot_at(c)]).then_inc(s_w_hi, 1)

            def weight_hi(dst, slot, count):
                act.wait_ge(s_landed[slot], 16 * count)
                copy_hi(dst, raw[:, slot]).then_inc(s_w_hi, 1)

            def hi_of(s_mm, s_hi, count, dst, src):
                act.wait_ge(s_mm, count)
                copy_hi(dst, src).then_inc(s_hi, 1)

            def value_dst(i, m):
                t0 = 2 * (m % 4)
                return vv[i][:, t0:t0 + 2, :]

            def exps_of(n):
                act.wait_ge(s_max_neg, n + 1)
                if due(n):
                    act.wait_ge(s_probs_ready, n)
                for b in range(HB):
                    a.activation(exps[:, b, :], scores_sb[:, b, :], ACT.Exp, bias=nmax[:, 1, b:b + 1],
                                 accum_out=esum[:, 0, b:b + 1]).then_inc(s_exp_done, 1)

            def first_hi(w, dst):
                act.wait_ge(s_landed[slot_at(w)], landed_count(w))
                copy_hi(dst, raw[:, slot_at(w)]).then_inc(s_w_hi, 1)

            for p in range(PC_INV + 1):
                dft_hi(p)
            lag0(0)
            lag0(1)
            dft_hi(PC_INV + 1)
            lag0(2)
            lag0(3)
            dft_hi(PC_INV + 2)
            for j in range(4):
                square(0, j)
            ctx_hi(0)
            ctx_hi(1)
            mirror(0)
            mirror(1)
            weigh(0)
            ctx_hi(2)
            mirror(2)
            weigh(1)
            scale_rows(0)
            mirror(3)
            weigh(2)
            scale_rows(1)
            ctx_hi(3)
            weigh(3)
            scale_rows(2)
            scale_rows(3)
            first_hi(PC_WV0, flat(wv[0]))
            first_hi(PC_QK00, flat(wqk[0][:, 0]))
            for j in range(4):
                square(1, j)
            first_hi(PC_QK01, flat(wqk[0][:, 1]))
            for tile in range(HB, B):
                lag0(tile)
            hi_of(s_k_mm, s_k_hi, 1, qk[0][:, 1], psK[:, :])
            normed_row(0)
            normed_row(1)
            hi_of(s_v_mm, s_v_hi, 1, value_dst(0, 0), psV[:, :].rearrange("p (b n) -> p b n", b=2))
            mirror(4)
            xt_hi(0)
            normed_row(2)
            mirror(5)
            xt_hi(1)
            normed_row(3)
            weigh(4)
            mirror(6)
            xt_hi(2)
            mirror(7)
            weigh(5)
            scale_rows(4)
            xt_hi(3)
            weigh(6)
            scale_rows(5)
            hi_of(s_v_mm, s_v_hi, 2, value_dst(0, 1), psV[:, :].rearrange("p (b n) -> p b n", b=2))
            weigh(7)
            scale_rows(6)
            scale_rows(7)
            hi_of(s_q_mm, s_q_hi, 1, qk[0][:, 0], psQ[:, :])
            double(0)
            double(1)
            exps_of(0)
            double(2)
            double(3)

            def ffn_hi(k):
                pc = DFT_PIECES + FFN0 + k
                act.wait_ge(s_landed[pc % SLOTS], 16 * (pc // SLOTS + 1))
                if k in UP or k in DOWN[:2]:
                    act.wait_ge(s_k_mm, units)
                if k in UP or k == FC1:
                    act.wait_ge(s_v_mm, units)
                if k == EXPERT or k in DOWN[2:]:
                    act.wait_ge(s_a_mm, units)
                copy_hi(ffn_dst(0, k), ffn_src(k)).then_inc(s_w_hi, 1)
                if k == EXPERT:
                    copy_hi(flat(gate[0]), raw[:, pc % SLOTS, LC * LAT:GX]).then_inc(s_gate_hi, 1)

            def pair_act(g):
                last = is_last(g)
                for j in range(4):
                    n = 4 * g + j
                    if j == 2:
                        k = 0 if last else 2
                        if due(8 * g):
                            act.wait_ge(s_o_mm, 8 * g)
                        weight_hi(flat(wo[0]), slot_of(g, k), rounds(g, k))
                    front = not (last and j == 3)
                    if front:
                        act.wait_ge(s_scores_mm, n + 1)
                        if is_first(g) and j == 1:
                            hi_of(s_k_mm, s_k_hi, n + 2, qk[0][:, 1], psK[:, :])
                        hi_of(s_q_mm, s_q_hi, n + 2, qk[0][:, 0], psQ[:, :])
                        if not (is_first(g) and j == 1):
                            hi_of(s_k_mm, s_k_hi, n + 2, qk[0][:, 1], psK[:, :])
                    if due(n):
                        act.wait_ge(s_a_mm, n)
                    hi_of(s_t_mm, s_t_hi, n + 1, flat(pt[0]), psT[:, :])
                    if is_first(g) and j == 0:
                        normed_row(4)
                        normed_row(5)
                    if j == 1 and not last:
                        act.wait_ge(s_k_mm, 4 * g + 3)
                        act.wait_ge(s_q_mm, 4 * g + 3)
                        weight_hi(flat(wqk[0][:, 0]), slot_of(g, 0), rounds(g, 0))
                    if j == 2 and not last:
                        act.wait_ge(s_k_mm, 4 * g + 4)
                        weight_hi(flat(wqk[0][:, 1]), slot_of(g, 3), rounds(g, 3))
                    if not (last and j >= 2):
                        if due(n - (1 if j % 2 else 0)):
                            act.wait_ge(s_a_mm, n - (1 if j % 2 else 0))
                        hi_of(s_v_mm, s_v_hi, n + 3, value_dst(0, j + 2), psV[:, :].rearrange("p (b n) -> p b n", b=2))
                    if j == 1 and not last:
                        act.wait_ge(s_v_mm, 4 * g + 4)
                        weight_hi(flat(wv[0]), slot_of(g, 1), rounds(g, 1))
                    if due(8 * g - 4 + (4 if j >= 2 else 0)):
                        act.wait_ge(s_o_mm, 8 * g - 4 + (4 if j >= 2 else 0))
                    hi_of(s_a_mm, s_a_hi, n + 1, heads_out(0, j), psA[:, :, 0])
                    if is_first(g) and j == 0:
                        xt_hi(4)
                        normed_row(6)
                        xt_hi(5)
                        normed_row(7)
                        xt_hi(6)
                        xt_hi(7)
                    if last and j == 2:
                        for k in UP:
                            ffn_hi(k)
                    if front:
                        exps_of(n + 1)
                    if is_first(g) and j == 0:
                        for tile in range(HB, B):
                            double(tile)

            every_pair(act, pair_act)

            def x2_hi(tile):
                act.wait_ge(s_x2_mm, tile + 1)
                if tile == 0:
                    act.wait_ge(s_q_mm, units)
                copy_hi(xn[0][:, :, tile_cols(tile)], banks[2 + tile % 2][:, :].rearrange("p (c n) -> p c n", c=DC)
                        ).then_inc(s_x2_hi, 1)

            def product_hi(s_mm, s_hi, hf, c, dst):
                act.wait_ge(s_mm, 2 * hf + c + 1)
                copy_hi(dst, banks[2 + c][:, :]).then_inc(s_hi, 1)

            def up_act(hf, c):
                n, bank = IC * hf + c, banks[c % 2]
                act.wait_ge(s_up_mm, n + 1)
                a.activation(bank[:, :], bank[:, :], ACT.Relu).then_inc(s_up_relu, 1)
                act.wait_ge(s_up_relu, n + 1)
                a.activation(bank[:, :], bank[:, :], ACT.Square).then_inc(s_up_sq, 1)
                act.wait_ge(s_up_sq, n + 1)
                if c >= 4:
                    act.wait_ge(s_down_mm, n - 3)
                elif hf == 1:
                    act.wait_ge(s_down_mm, IC)
                if n == 0:
                    act.wait_ge(s_o_mm, 2 * units)
                copy_hi(hidden(0, c), bank[:, :]).then_inc(s_up_hi, 1)

            def logits_copy(hf):
                act.wait_ge(s_lg_mm, hf + 1)
                if hf == 0:
                    act.wait_ge(s_a_lo, units)
                else:
                    act.wait_ge(s_lg_turned, hf)
                a.activation(flat(rest)[0:NE, :], banks[2][0:NE, :], ACT.Copy).then_inc(s_lg_copied, 1)

            def routed_scale(hf, b):
                tile = HB * hf + b
                act.wait_ge(s_r_mm, tile + 1)
                act.wait_ge(s_route, tile + 1)
                if hf == 1:
                    act.wait_ge(s_w_sum, b + 1)
                a.activation(flat(smx[:, b]), banks[2 + b % 2][:, :], ACT.Copy, scale=rsum[:, tile, :]
                             ).then_inc(s_r_scaled, 1)

            def last_norm(tile):
                act.wait_ge(s_w_shift, tile + 1)
                a.activation(acc[:, tile, :], acc[:, tile, :], ACT.Identity, bias=stat[:, tile, 5:6],
                             scale=stat[:, tile, 3:4]).then_inc(s_out_ready, 1)

            x2_hi(0)
            x2_hi(1)
            ffn_hi(FC1)
            x2_hi(2)
            x2_hi(3)
            ffn_hi(EXPERT)
            for hf in range(2):
                up_act(hf, 0)
                if hf == 0:
                    ffn_hi(FC2)
                if due(2 * hf):
                    act.wait_ge(s_ex_mm, 2 * hf)
                for c in range(LC):
                    product_hi(s_xl_mm, s_xl_hi, hf, c, qk[0][:, c])
                if hf == 0:
                    ffn_hi(DOWN[0])
                up_act(hf, 1)
                if due(HB * hf):
                    act.wait_ge(s_r_mm, HB * hf)
                for c in range(LC):
                    product_hi(s_ex_mm, s_ex_hi, hf, c, wo[0][:, c])
                if hf == 0:
                    ffn_hi(DOWN[1])
                logits_copy(hf)
                for c in range(2, IC):
                    up_act(hf, c)
                    if hf == 0 and c in (2, 3):
                        ffn_hi(DOWN[c])
                    if hf == 0 and c in (3, 4):
                        x2_hi(2 * c - 2)
                        x2_hi(2 * c - 1)
                    if hf == 1 and c in (3, 4):
                        last_norm(2 * c - 6)
                        last_norm(2 * c - 5)
                    if c == 5:
                        routed_scale(hf, 0)
                        routed_scale(hf, 1)
                    if c >= 6:
                        routed_scale(hf, c - 4)
            for tile in range(HB, B):
                last_norm(tile)

        @block.vector
        def _(dve):
            v = nc.vector

            def lo_part(dst, src, hi):
                return v.tensor_tensor(dst, src, hi, ALU.subtract)

            def dft_lo(p):
                dve.wait_ge(s_dft_hi, p + 1)
                lo_part(dft_dst(1, p), raw2(p % SLOTS), dft_dst(0, p)).then_inc(s_dft_lo, 1)

            def square_lo(hf, j):
                dve.wait_ge(s_sq_hi, 4 * hf + j + 1)
                lo_part(sq(1)[:, j], banks[j][:, :], sq(0)[:, j]).then_inc(s_sq_lo, 1)

            def top(tile):
                corr = banks[4 + tile % 4]
                dve.wait_ge(s_mirrored, tile + 1)
                v.max(topv[:, tile, 1:9], corr[:, 0:D - 1]).then_inc(s_top_val, 1)
                dve.wait_ge(s_top_val, tile + 1)
                dve.wait_ge(s_lag0, tile + 1)
                v.tensor_reduce(topm[:, tile, 0:1], topv[:, tile, 0:LAGS], AX.X, ALU.max).then_inc(s_top_max, 1)
                v.max_index(topi[:, tile, :], topv[:, tile, 1:9], corr[:, 0:D - 1]).then_inc(s_top_idx, 1)
                dve.wait_ge(s_top_max, 2 * tile + 1)
                v.tensor_scalar(topm[:, tile, 1:2], topm[:, tile, 0:1], -1.0, None, ALU.mult).then_inc(s_top_max, 1)
                dve.wait_ge(s_top_idx, tile + 1)
                v.tensor_scalar(gidx[:, tile, :], topi[:, tile, :], rowbase[:, :], float(tile * P * 2 * D),
                                ALU.add, ALU.add).then_inc(s_gather_idx, 1)

            def weights(tile):
                dve.wait_ge(s_w_exp, tile + 1)
                v.reciprocal(topm[:, tile, 2:3], wsum[:, tile, 0:1]).then_inc(s_w_rec, 1)
                dve.wait_ge(s_w_rec, tile + 1)
                v.tensor_scalar(wsum[:, tile, 1:2], wts[:, tile, 0:1], topm[:, tile, 2:3], 1.0, ALU.mult, ALU.add
                                ).then_inc(s_w0_ready, 1)
                v.tensor_scalar(wts[:, tile, 1:LAGS], wts[:, tile, 1:LAGS], topm[:, tile, 2:3], None, ALU.mult
                                ).then_inc(s_w_ready, 1)

            def other_weights(hf):
                dve.wait_ge(s_w_ready, HB * hf + HB)
                v.tensor_reduce(others[:, hf:hf + 1], wts[:, HB * hf:HB * hf + HB, 1:LAGS], AX.XY, ALU.add
                                ).then_inc(s_others, 1)
                dve.wait_ge(s_others, hf + 1)
                v.tensor_scalar(nonzero[:, hf:hf + 1], others[:, hf:hf + 1], 0.0, None, ALU.not_equal
                                ).then_inc(s_nonzero, 1)

            def delays_sum(hf):
                dve.wait_ge(s_count_mm, hf + 1)
                v.tensor_scalar(general[0:1, hf:hf + 1], banks[4 + hf][0:1, 0:1], 0.0, None,
                                ALU.not_equal).then_inc(s_general, 1)
                dve.wait_ge(s_general, hf + 1)
                dve.wait_ge(s_acc_scaled, HB * hf + HB)
                dve.wait_ge(s_gather_idx, HB * hf + HB)
                count = dve.value_load(general[0:1, hf:hf + 1], min_val=0, max_val=1)
                with dve.If(count != 0):
                    for n in range(HB * (LAGS - 1)):
                        tile, k = HB * hf + n // (LAGS - 1), n % (LAGS - 1)
                        dve.wait_ge(s_got[hf][n % RING], 16 * (n // RING + 1))
                        if n % (LAGS - 1):
                            dve.wait_ge(s_acc_sum[hf], n)
                        v.scalar_tensor_tensor(acc[:, tile, :], shifted(hf, n), wts[:, tile, k + 1:k + 2],
                                               acc[:, tile, :], ALU.mult, ALU.add).then_inc(s_acc_sum[hf], 1)
                    dve.wait_ge(s_acc_sum[hf], HB * (LAGS - 1))

            def stats(tile):
                v.bn_stats(st6[:, tile, :], acc[:, tile, :]).then_inc(s_stats_a, 1)
                dve.wait_ge(s_stats_a, tile + 1)
                v.bn_aggr(mv[:, tile, :], st6[:, tile, :]).then_inc(s_stats_b, 1)

            def xt_lo(tile):
                dve.wait_ge(s_xt_hi, tile + 1)
                part = slice(tile * P, (tile + 1) * P)
                lo_part(xn[1][:, :, part], turned(tile), xn[0][:, :, part]).then_inc(s_xt_lo, 1)

            def lo_of(s_hi, s_lo, count, dst, src, hi):
                dve.wait_ge(s_hi, count)
                lo_part(dst, src, hi).then_inc(s_lo, 1)

            def value_dst(i, m):
                t0 = 2 * (m % 4)
                return vv[i][:, t0:t0 + 2, :]

            def softmax_in(n):
                dve.wait_ge(s_scores_mm, n + 1)
                dve.wait_ge(s_bm_ready, n + 1)
                if due(4 * n):
                    dve.wait_ge(s_exp_done, 4 * n)
                v.tensor_tensor(scores_sb, psS[:, :, 0], bm, ALU.add).then_inc(s_scores_sum, 1)
                dve.wait_ge(s_scores_sum, n + 1)
                v.tensor_tensor(scores_sb, psS[:, :, 1], scores_sb, ALU.add).then_inc(s_scores_full, 1)
                dve.wait_ge(s_scores_full, n + 1)
                v.tensor_reduce(nmax[:, 0, :], scores_sb, AX.X, ALU.max).then_inc(s_scores_max, 1)
                dve.wait_ge(s_scores_max, n + 1)
                v.tensor_scalar(nmax[:, 1, :], nmax[:, 0, :], -0.5 * FAR, -1.0, ALU.max, ALU.mult
                                ).then_inc(s_max_neg, 1)

            def softmax_out(n):
                dve.wait_ge(s_exp_done, 4 * n + 4)
                v.tensor_scalar(esum[:, 1, :], esum[:, 0, :], 1e-30, None, ALU.max).then_inc(s_sum_clamped, 1)
                dve.wait_ge(s_sum_clamped, n + 1)
                v.reciprocal(esum[:, 2, :], esum[:, 1, :]).then_inc(s_sum_inverse, 1)
                dve.wait_ge(s_sum_inverse, n + 1)
                if due(n):
                    dve.wait_ge(s_t_mm, n)
                v.tensor_tensor(probs, exps, esum[:, 2, :].unsqueeze(2).to_broadcast([P, HB, P]), ALU.mult
                                ).then_inc(s_probs_ready, 1)

            def attended(n, j):
                dve.wait_ge(s_a_hi, n + 1)
                v.tensor_tensor(rest[:, :, :], psA[:, :, 0], heads_out(0, j), ALU.subtract).then_inc(s_a_rest, 1)
                dve.wait_ge(s_a_rest, n + 1)
                v.tensor_tensor(heads_out(1, j), psA[:, :, 1], rest[:, :, :], ALU.add).then_inc(s_a_lo, 1)

            def add_out(o, i, tile):
                dve.wait_ge(s_o_mm, 2 * o + i + 1)
                v.tensor_tensor(acc[:, tile, :], out_banks(o)[i][:, :], acc[:, tile, :], ALU.add).then_inc(s_o_add, 1)

            for p in range(PC_INV + 3):
                dft_lo(p)
            dve.wait_ge(s_mask_landed, 16)
            v.tensor_scalar(far[:, :, :], m8[:, :, :], -1.0, FAR, ALU.add, ALU.mult).then_inc(s_far_ready, 1)
            for j in range(4):
                square_lo(0, j)
            dve.wait_ge(s_consts, 5)
            top(0)
            top(1)
            weights(0)
            top(2)
            weights(1)
            top(3)
            weights(2)
            weights(3)
            other_weights(0)
            delays_sum(0)
            stats(0)
            stats(1)
            square_lo(1, 0)
            square_lo(1, 1)
            stats(2)
            stats(3)
            square_lo(1, 2)
            square_lo(1, 3)
            lo_of(s_k_hi, s_k_lo, 1, qk[1][:, 1], psK[:, :], qk[0][:, 1])
            lo_of(s_v_hi, s_v_lo, 1, value_dst(1, 0), psV[:, :].rearrange("p (b n) -> p b n", b=2), value_dst(0, 0))
            top(4)
            xt_lo(0)
            top(5)
            xt_lo(1)
            weights(4)
            top(6)
            xt_lo(2)
            weights(5)
            top(7)
            xt_lo(3)
            weights(6)
            lo_of(s_v_hi, s_v_lo, 2, value_dst(1, 1), psV[:, :].rearrange("p (b n) -> p b n", b=2), value_dst(0, 1))
            weights(7)
            other_weights(1)
            lo_of(s_q_hi, s_q_lo, 1, qk[1][:, 0], psQ[:, :], qk[0][:, 0])
            delays_sum(1)
            stats(4)
            softmax_in(0)
            stats(5)
            softmax_out(0)
            stats(6)
            stats(7)

            def ffn_lo(k):
                dve.wait_ge(s_w_hi, FFN0 + k + 1)
                lo_part(ffn_dst(1, k), ffn_src(k), ffn_dst(0, k)).then_inc(s_f_lo, 1)
                if k == EXPERT:
                    dve.wait_ge(s_gate_hi, 1)
                    slot = (DFT_PIECES + FFN0 + k) % SLOTS
                    lo_part(flat(gate[1]), raw[:, slot, LC * LAT:GX], flat(gate[0])).then_inc(s_gate_lo, 1)

            def y_stats(tile):
                dve.wait_ge(s_o_add, 2 * (units - 4) + tile + 1)
                v.bn_stats(st6[:, tile, :], acc[:, tile, :]).then_inc(s_y_stats_a, 1)
                dve.wait_ge(s_y_stats_a, tile + 1)
                v.bn_aggr(mv[:, tile, :], st6[:, tile, :]).then_inc(s_y_stats_b, 1)

            def x2(tile):
                dve.wait_ge(s_y_rstd, tile + 1)
                v.tensor_scalar(acc[:, tile, :], acc[:, tile, :], mv[:, tile, 0:1], stat[:, tile, 1:2],
                                ALU.subtract, ALU.mult).then_inc(s_x2_ready, 1)

            def pair_dve(g):
                last = is_last(g)
                for j in range(4):
                    n = 4 * g + j
                    front = not (last and j == 3)
                    if front:
                        if is_first(g) and j == 1:
                            lo_of(s_k_hi, s_k_lo, n + 2, qk[1][:, 1], psK[:, :], qk[0][:, 1])
                        lo_of(s_q_hi, s_q_lo, n + 2, qk[1][:, 0], psQ[:, :], qk[0][:, 0])
                        if not (is_first(g) and j == 1):
                            lo_of(s_k_hi, s_k_lo, n + 2, qk[1][:, 1], psK[:, :], qk[0][:, 1])
                    if last and j == 3:
                        y_stats(0)
                    lo_of(s_t_hi, s_t_lo, n + 1, flat(pt[1]), psT[:, :], flat(pt[0]))
                    if last and j == 3:
                        y_stats(1)
                        add_out(n - 2, 0, 2)
                        x2(0)
                        add_out(n - 2, 1, 3)
                        x2(1)
                        y_stats(2)
                    if not (last and j >= 2):
                        lo_of(s_v_hi, s_v_lo, n + 3, value_dst(1, j + 2), psV[:, :].rearrange("p (b n) -> p b n", b=2),
                              value_dst(0, j + 2))
                    attended(n, j)
                    if is_first(g) and j == 0:
                        xt_lo(4)
                        xt_lo(5)
                    if front:
                        softmax_in(n + 1)
                    if is_first(g) and j == 0:
                        xt_lo(6)
                        xt_lo(7)
                    if not (isinstance(g, int) and g == 0 and j < 2):
                        for i in range(2):
                            if not (last and j == 3):
                                add_out(n - 2, i, (2 * ((j + 2) % 4) + i) % B)
                            if last and j == 2 and i == 0:
                                ffn_lo(UP[3])
                            if front and i == 0:
                                softmax_out(n + 1)
                    elif front:
                        softmax_out(n + 1)

            every_pair(dve, pair_dve)

            def x2_lo(tile):
                dve.wait_ge(s_x2_hi, tile + 1)
                lo_part(xn[1][:, :, tile_cols(tile)], banks[2 + tile % 2][:, :].rearrange("p (c n) -> p c n", c=DC),
                        xn[0][:, :, tile_cols(tile)]).then_inc(s_x2_lo, 1)

            def product_lo(s_hi, s_lo, hf, c, dst):
                dve.wait_ge(s_hi, 2 * hf + c + 1)
                lo_part(dst[1][:, c], banks[2 + c][:, :], dst[0][:, c]).then_inc(s_lo, 1)

            def up_lo(hf, c):
                dve.wait_ge(s_up_hi, IC * hf + c + 1)
                lo_part(hidden(1, c), banks[c % 2][:, :], hidden(0, c)).then_inc(s_up_lo, 1)

            def route(hf):
                dve.wait_ge(s_lg_turned, hf + 1)
                for i in range(HB):
                    v.max(lg8[:, HB * hf + i, :], banks[3][:, i * NE:(i + 1) * NE]).then_inc(s_lg_top, 1)
                dve.wait_ge(s_lg_top, HB * hf + HB)
                for i in range(HB):
                    tile = HB * hf + i
                    v.tensor_tensor(rsum[:, tile, :], lg8[:, tile, 0:1], lg8[:, tile, 1:2], ALU.add
                                    ).then_inc(s_route, 1)

            def u_sum(tile):
                u = flat(smx[:, tile % 4])
                dve.wait_ge(s_r_scaled, tile + 1)
                dve.wait_ge(s_down_mm, IC * (tile // HB) + 4 + tile % HB + 1)
                v.tensor_tensor(u, banks[4 + tile % HB][:, :], u, ALU.add).then_inc(s_u_ready, 1)
                dve.wait_ge(s_u_ready, tile + 1)
                v.bn_stats(st6[:, tile, :], u).then_inc(s_u_stats_a, 1)
                dve.wait_ge(s_u_stats_a, tile + 1)
                v.bn_aggr(mv[:, tile, :], st6[:, tile, :]).then_inc(s_u_stats_b, 1)

            def residual(tile):
                u = flat(smx[:, tile % 4])
                dve.wait_ge(s_u_stats_b, tile + 1)
                v.scalar_tensor_tensor(u, u, mv[:, tile, 0:1], rows[:, 0], ALU.subtract, ALU.mult
                                       ).then_inc(s_u_gamma, 1)
                dve.wait_ge(s_x2_beta, tile + 1)
                dve.wait_ge(s_u_rstd, tile + 1)
                dve.wait_ge(s_u_gamma, tile + 1)
                v.scalar_tensor_tensor(acc[:, tile, :], u, stat[:, tile, 1:2], acc[:, tile, :], ALU.mult, ALU.add
                                       ).then_inc(s_w_sum, 1)
                dve.wait_ge(s_w_sum, tile + 1)
                v.bn_stats(st6[:, tile, :], acc[:, tile, :]).then_inc(s_w_stats_a, 1)
                dve.wait_ge(s_w_stats_a, tile + 1)
                v.bn_aggr(mv[:, tile, :], st6[:, tile, :]).then_inc(s_w_stats_b, 1)

            y_stats(3)
            x2(2)
            x2_lo(0)
            x2(3)
            x2_lo(1)
            for i in range(2):
                add_out(units - 2, i, 4 + i)
            x2_lo(2)
            x2_lo(3)
            for i in range(2):
                add_out(units - 1, i, 6 + i)
            ffn_lo(EXPERT)
            for hf in range(2):
                up_lo(hf, 0)
                if hf == 1:
                    residual(0)
                for c in range(LC):
                    product_lo(s_xl_hi, s_xl_lo, hf, c, [qk[0], qk[1]])
                if hf == 0:
                    for tile in range(HB, B):
                        y_stats(tile)
                    ffn_lo(FC2)
                else:
                    residual(1)
                up_lo(hf, 1)
                for c in range(LC):
                    product_lo(s_ex_hi, s_ex_lo, hf, c, [wo[0], wo[1]])
                if hf == 0:
                    ffn_lo(DOWN[1])
                    for tile in range(HB, B):
                        x2(tile)
                else:
                    residual(2)
                    residual(3)
                up_lo(hf, 2)
                route(hf)
                up_lo(hf, 3)
                if hf == 0:
                    ffn_lo(DOWN[3])
                    x2_lo(4)
                    x2_lo(5)
                up_lo(hf, 4)
                if hf == 0:
                    x2_lo(6)
                    x2_lo(7)
                for c in range(5, IC):
                    up_lo(hf, c)
                for tile in range(HB * hf, HB * hf + HB):
                    u_sum(tile)
                    if tile > HB:
                        residual(tile - 1)
            residual(B - 1)

        @block.tensor
        def _(pe):
            mm = nc.tensor.matmul

            def mm3(out, lhs, rhs, first, last):
                mm(out, lhs(0), rhs(1), start=first, stop=False)
                mm(out, lhs(1), rhs(0), start=False, stop=False)
                return mm(out, lhs(0), rhs(0), start=False, stop=last)

            def mm_parts(out, lhs, rhs_both, rhs_hi):
                mm(out, lhs(0), rhs_both, start=True, stop=False)
                return mm(out[:, 1], lhs(1), rhs_hi, start=False, stop=True)

            def dft(hf):
                if hf == 1:
                    pe.wait_ge(s_sq_lo, 4)
                for cc in range(2):
                    pe.wait_ge(s_dft_lo, (2 + 2 * cc) if hf == 0 else (PC_INV + 2 + cc))
                    for j in range(4):
                        for c in (2 * cc, 2 * cc + 1):
                            last = mm3(banks[j][:, :], lambda i: dftC[i][:, c, j * P:(j + 1) * P],
                                       lambda i: dftX(i, hf)[:, c, :], c == 0, c == DC - 1)
                        if cc == 1:
                            last.then_inc(s_dft_mm, 1)
                        if cc == 1 and j == 1 and hf == 1:
                            count_general(0)

            def corr(tile):
                if tile == 0:
                    pe.wait_ge(s_dft_lo, PC_INV + 1)
                pe.wait_ge(s_sq_lo, 4 * (tile // HB) + 4)
                if tile >= 4:
                    pe.wait_ge(s_top_idx, tile - 3)
                if tile == 4:
                    pe.wait_ge(s_general, 1)
                lt = slice((tile % HB) * P, (tile % HB + 1) * P)
                for j in range(4):
                    last = mm3(banks[4 + tile % 4][:, 0:LAST_LAG], lambda i: sq(i)[:, j, lt],
                               lambda i: dftD[i][:, j, :], j == 0, j == 3)
                last.then_inc(s_corr_mm, 1)

            def count_general(hf):
                pe.wait_ge(s_nonzero, hf + 1)
                out = banks[4 + hf][0:1, 0:1]
                pe.wait_ge(s_top_idx, HB * hf + HB)
                nc.tensor.matmul(out, nonzero[:, hf:hf + 1], ones[:, :], start=True, stop=True).then_inc(s_count_mm, 1)

            def warm_up():
                pe.wait_ge(s_consts, 5)
                for _ in range(WARM_UPS):
                    nc.tensor.transpose(banks[7][:, 0:P], ident[:, :], ident[:, :])

            def transposes(tile):
                pe.wait_ge(s_xn_ready, tile + 1)
                if tile == 0:
                    pe.wait_ge(s_sq_lo, 8)
                elif tile == HB:
                    pe.wait_ge(s_t_lo, 1)
                elif tile == HB + 1:
                    pe.wait_ge(s_q_lo, 2)
                if tile >= 2:
                    pe.wait_ge(s_xt_lo, tile - 1)
                out = turned(tile)
                for c in range(DC):
                    last = nc.tensor.transpose(out[:, c], rows[:, tile % 2, c * P:(c + 1) * P], ident[:, :])
                last.then_inc(s_xt_mm, 1)

            def project(which, n, g, j):
                hp, hf = j % 2, j // 2
                if isinstance(g, int):
                    pe.wait_ge(*low_done(piece_qk(g, hp)))
                else:
                    pe.wait_ge(s_w_lo, piece_qk(g, hp) + 1)
                if which == 1 and isinstance(n, int) and n == 0:
                    pe.wait_ge(s_w_lo, CTX_PIECES)
                if which == 0 and isinstance(n, int) and n in (0, 2):
                    pe.wait_ge(s_xt_lo, HB if n == 0 else B)
                if isinstance(n, int) and n == 0:
                    pe.wait_ge(s_sq_lo, 5 + which)
                src = (xn, cx)[which]
                out = (psQ, psK)[which]
                if due(n):
                    pe.wait_ge((s_q_lo, s_k_lo)[which], n)
                if which == 1 and due(2 * n - 7):
                    pe.wait_ge(s_o_add, 2 * n - 7)
                for c in range(DC):
                    last = mm3(out[:, :], lambda i: wqk[i][:, hp, which, c, :],
                               lambda i: src[i][:, c, hf * HALF:(hf + 1) * HALF], c == 0, c == DC - 1)
                last.then_inc((s_q_mm, s_k_mm)[which], 1)

            def values(m, g, first_tile):
                if isinstance(g, int):
                    pe.wait_ge(*low_done(piece_wv(g)))
                else:
                    pe.wait_ge(s_w_lo, piece_wv(g) + 1)
                if due(m):
                    pe.wait_ge(s_v_lo, m)
                else:
                    pe.wait_ge(s_sq_lo, 8)
                if due(2 * m - 8):
                    pe.wait_ge(s_o_add, 2 * m - 8)
                for i in range(2):
                    tk = slice((first_tile + i) * P, (first_tile + i + 1) * P)
                    for c in range(DC):
                        last = mm3(psV[:, i * 2 * P:(i + 1) * 2 * P], lambda i_: cx[i_][:, c, tk],
                                   lambda i_: wv[i_][:, c, :], c == 0, c == DC - 1)
                last.then_inc(s_v_mm, 1)

            def scores(n):
                pe.wait_ge(s_q_lo, n + 1)
                pe.wait_ge(s_k_lo, n + 1)
                if due(n):
                    pe.wait_ge(s_scores_full, n)
                else:
                    pe.wait_ge(s_top_idx, B)
                for b in range(HB):
                    bk = slice(b * P, (b + 1) * P)
                    last = mm_parts(psS[:, b], lambda i: qk[i][:, 0, bk], qk_parts[:, :, 1, bk], qk[0][:, 1, bk])
                last.then_inc(s_scores_mm, 1)

            def turn_probs(n):
                pe.wait_ge(s_probs_ready, n + 1)
                if due(n):
                    pe.wait_ge(s_t_lo, n)
                if isinstance(n, int) and n < 2:
                    pe.wait_ge(s_xt_lo, (HB, B)[n])
                for b in range(HB):
                    last = nc.tensor.transpose(psT[:, b * P:(b + 1) * P], probs[:, b, :], ident[:, :])
                last.then_inc(s_t_mm, 1)

            def attend(n, g, j):
                hp, hf = j % 2, j // 2
                pe.wait_ge(s_t_lo, n + 1)
                if due(4 * g + 2 + 2 * hf):
                    pe.wait_ge(s_v_lo, 4 * g + 2 + 2 * hf)
                if due(n):
                    pe.wait_ge(s_a_lo, n)
                else:
                    pe.wait_ge(s_general, 2)
                for b in range(HB):
                    last = mm_parts(psA[:, b], lambda i: vv[i][:, HB * hf + b, hp * P:(hp + 1) * P],
                                    pt_parts[:, :, b, :], pt[0][:, b, :])
                last.then_inc(s_a_mm, 1)

            def outputs(o, g, first_tile):
                hf = first_tile // HB
                if isinstance(g, int):
                    pe.wait_ge(*low_done(piece_wo(g)))
                else:
                    pe.wait_ge(s_w_lo, piece_wo(g) + 1)
                if due(4 * g + 2 + 2 * hf):
                    pe.wait_ge(s_a_lo, 4 * g + 2 + 2 * hf)
                for i in range(2):
                    lt = slice(((first_tile + i) % HB) * P, ((first_tile + i) % HB + 1) * P)
                    if isinstance(o, int) and o in LATE:
                        pe.wait_ge(s_q_lo, units)
                        pe.wait_ge(s_k_lo, units)
                        pe.wait_ge(s_scores_full, units)
                        pe.wait_ge(s_o_add, 2 * (o - 2) + i + 1)
                    else:
                        if i == 0:
                            pe.wait_ge(s_k_lo, min(o + 4, units) if isinstance(o, int) else o + 4)
                        else:
                            pe.wait_ge(s_v_lo, min(o + 5, units) if isinstance(o, int) else o + 5)
                        if isinstance(o, int) and due(2 * (o - 1) + i + 1):
                            pe.wait_ge(s_o_add, 2 * (o - 1) + i + 1)
                    for hp in range(2):
                        last = mm3(out_banks(o)[i][:, :], lambda i_: at[i_][:, hf, hp, lt], lambda i_: wo[i_][:, hp, :],
                                   hp == 0, hp == 1)
                    last.then_inc(s_o_mm, 1)

            warm_up()
            dft(0)
            for tile in range(HB):
                corr(tile)
            dft(1)
            project(1, 0, 0, 0)
            values(0, 0, 0)
            for tile in range(HB):
                corr(HB + tile)
                transposes(tile)
            values(1, 0, 2)
            project(0, 0, 0, 0)
            count_general(1)
            scores(0)

            def pair_pe(g):
                last = is_last(g)
                for j in range(4):
                    n = 4 * g + j
                    front = not (last and j == 3)
                    if front:
                        for which in ((1, 0) if is_first(g) and j == 1 else (0, 1)):
                            project(which, n + 1, *nxt(g, j))
                    if last and j == 3:
                        outputs(n - 2, g, 2)
                    turn_probs(n)
                    if not (last and j >= 2):
                        values(n + 2, g + (j >= 2), (2 * j + 4) % B)
                    attend(n, g, j)
                    if is_first(g) and j == 0:
                        transposes(HB)
                        transposes(HB + 1)
                    if front:
                        scores(n + 1)
                    if is_first(g) and j == 0:
                        transposes(HB + 2)
                        transposes(HB + 3)
                    if not (isinstance(g, int) and (g == 0 and j < 2 or last and j == 3)):
                        outputs(n - 2, g - (j < 2), (2 * j + 4) % B)

            every_pair(pe, pair_pe)

            def x2_transposes(tile):
                pe.wait_ge(s_x2_ready, tile + 1)
                if tile == 0:
                    pe.wait_ge(s_t_lo, units)
                    pe.wait_ge(s_v_lo, units)
                    pe.wait_ge(s_o_add, 2 * (units - 3))
                elif tile == HB:
                    pe.wait_ge(s_lg_copied, 1)
                elif tile == HB + 1:
                    pe.wait_ge(s_route, HB)
                elif tile > 1:
                    pe.wait_ge(s_x2_lo, tile - 1)
                for c in range(DC):
                    last = nc.tensor.transpose(banks[2 + tile % 2][:, c * P:(c + 1) * P],
                                               acc[:, tile, c * P:(c + 1) * P], ident[:, :])
                last.then_inc(s_x2_mm, 1)

            def x_latent(hf):
                pe.wait_ge(*low_done(FFN0 + FC1))
                pe.wait_ge(s_x2_lo, HB * hf + HB)
                if hf == 1:
                    pe.wait_ge(s_r_scaled, HB)
                for o in range(LC):
                    for c in range(DC):
                        last = mm3(banks[2 + o][:, :], lambda i: wv[i][:, c, tile_cols(o)],
                                   lambda i: xn[i][:, c, half_cols(hf)], c == 0, c == DC - 1)
                    last.then_inc(s_xl_mm, 1)

            def up(hf, o):
                n = IC * hf + o
                if n == 0:
                    pe.wait_ge(s_q_lo, units)
                    pe.wait_ge(s_k_lo, units)
                    pe.wait_ge(s_o_add, 2 * units)
                    pe.wait_ge(s_x2_lo, HB)
                    for k in UP:
                        pe.wait_ge(*low_done(FFN0 + k))
                if due(n - 1):
                    pe.wait_ge(s_up_lo, n - 1)
                for c in range(DC):
                    last = mm3(banks[o % 2][:, :], lambda i: cx[i][:, c, tile_cols(o)],
                               lambda i: xn[i][:, c, half_cols(hf)], c == 0, c == DC - 1)
                last.then_inc(s_up_mm, 1)

            def expert_out(hf):
                pe.wait_ge(*low_done(FFN0 + EXPERT))
                pe.wait_ge(s_xl_lo, LC * (hf + 1))
                for o in range(LC):
                    for c in range(LC):
                        last = mm3(banks[2 + o][:, :], lambda i: expert[i][:, c, tile_cols(o)],
                                   lambda i: qk[i][:, c, :], c == 0, c == LC - 1)
                    last.then_inc(s_ex_mm, 1)

            def logits(hf):
                pe.wait_ge(s_gate_lo, 1)
                pe.wait_ge(s_ex_lo, LC * (hf + 1))
                for c in range(DC):
                    last = mm3(banks[2][0:NE, :], lambda i: gate[i][:, c, :],
                               lambda i: xn[i][:, c, half_cols(hf)], c == 0, c == DC - 1)
                last.then_inc(s_lg_mm, 1)

            def turn_logits(hf):
                pe.wait_ge(s_lg_copied, hf + 1)
                for b in range(HB):
                    last = nc.tensor.transpose(banks[3][:, b * NE:(b + 1) * NE],
                                               flat(rest)[0:NE, tile_cols(b)], ident[0:NE, 0:NE])
                last.then_inc(s_lg_turned, 1)

            def down_part(c, b):
                return mm3(banks[4 + b][:, :], lambda i: hidden(i, c)[:, tile_cols(b)],
                           lambda i: wdown[i][c // 4][:, c % 4, :], c == 0, c == IC - 1)

            def down(hf, c):
                if hf == 0 and c % 2 == 0:
                    pe.wait_ge(*low_done(FFN0 + DOWN[c // 2]))
                pe.wait_ge(s_up_lo, IC * hf + c + 1)
                if c == 0 and hf == 0:
                    pe.wait_ge(s_a_lo, units)
                    pe.wait_ge(s_o_add, 2 * units)
                for b in range(HB):
                    if c == 0 and hf == 1:
                        pe.wait_ge(s_u_ready, b + 1)
                    last = down_part(c, b)
                last.then_inc(s_down_mm, 1)

            def down_rest(hf):
                if hf == 0:
                    pe.wait_ge(*low_done(FFN0 + DOWN[2]))
                    pe.wait_ge(*low_done(FFN0 + DOWN[3]))
                for b in range(HB):
                    for c in range(4, IC):
                        if b == 0:
                            pe.wait_ge(s_up_lo, IC * hf + c + 1)
                        last = down_part(c, b)
                    last.then_inc(s_down_mm, 1)

            def routed(hf, b):
                tile = HB * hf + b
                if b == 0:
                    pe.wait_ge(*low_done(FFN0 + FC2))
                    pe.wait_ge(s_ex_lo, LC * (hf + 1))
                if b >= 2:
                    pe.wait_ge(s_r_scaled, tile - 1)
                elif hf == 0:
                    pe.wait_ge(s_x2_lo, B)
                else:
                    pe.wait_ge(s_lg_copied, hf + 1)
                    pe.wait_ge(s_route, B)
                for c in range(LC):
                    last = mm3(banks[2 + b % 2][:, :], lambda i: wo[i][:, c, tile_cols(b)],
                               lambda i: ext[i][:, c, :], c == 0, c == LC - 1)
                last.then_inc(s_r_mm, 1)

            x2_transposes(0)
            x2_transposes(1)
            outputs(units - 2, PAIRS - 1, 4)
            x2_transposes(2)
            x2_transposes(3)
            outputs(units - 1, PAIRS - 1, 6)
            for hf in range(2):
                up(hf, 0)
                x_latent(hf)
                up(hf, 1)
                expert_out(hf)
                down(hf, 0)
                logits(hf)
                up(hf, 2)
                turn_logits(hf)
                for c in (1, 2):
                    down(hf, c)
                    up(hf, c + 2)
                    if hf == 0:
                        x2_transposes(2 * c + 2)
                        x2_transposes(2 * c + 3)
                down(hf, 3)
                up(hf, 5)
                routed(hf, 0)
                routed(hf, 1)
                up(hf, 6)
                routed(hf, 2)
                up(hf, 7)
                routed(hf, 3)
                down_rest(hf)


def layouts(i):
    x = np.asarray(i["x"])
    n = np.arange(D)
    f = np.arange(D // 2)
    ang = 2 * np.pi * np.outer(n, f) / D
    fwd = np.concatenate([np.cos(ang), np.sin(ang)], axis=1)
    fwd[:, D // 2] = np.cos(np.pi * n)
    lag = np.arange(1, LAST_LAG + 1)
    wave = np.cos(2 * np.pi * np.outer(f, lag) / D)
    inv = np.concatenate([wave, wave], axis=0) * 2 / D
    inv[0] /= 2
    inv[D // 2] = np.cos(np.pi * lag) / D
    chunks = lambda m: m.reshape(DC, P, -1).transpose(1, 0, 2)
    two = lambda m: [m[:, 0:2].reshape(P, PIECE), m[:, 2:4].reshape(P, PIECE)]
    C, Dm = chunks(fwd.astype(np.float32)), chunks(inv.astype(np.float32))
    xT = chunks(np.ascontiguousarray(x.reshape(TOK, D).T))
    c0, c1 = two(C)
    a0, a1 = two(xT[:, :, :HALF])
    b0, b1 = two(xT[:, :, HALF:])
    ctxT = np.asarray(i["ctx_4096"]).reshape(TOK, D).T.reshape(DC, P, TOK)
    xf = x.reshape(TOK, D)
    by_chunk = lambda w: np.asarray(w).reshape(-1, P, w.shape[1]).transpose(1, 0, 2).reshape(P, -1)
    up = np.asarray(i["L0_ffn_up_w"])
    down = np.asarray(i["L0_ffn_down_w"]).reshape(4, 2, P, D).transpose(0, 2, 1, 3).reshape(4, P, PIECE)
    fc1, fc2 = by_chunk(i["L0_ffn_fc1_w"]), by_chunk(i["L0_ffn_fc2_w"])
    gx = np.concatenate([by_chunk(i["L0_ffn_expert_w"]), by_chunk(i["L0_ffn_gate_w"])], axis=1)
    heads = lambda w: np.asarray(w).reshape(H, P, DC, P).transpose(0, 3, 2, 1)
    return {
        "dft": np.stack([c0, a0, c1, a1, Dm.reshape(P, PIECE), b0, b1]),
        "x": xf,
        "xx": np.concatenate([xf, xf], axis=1).reshape(-1, 1),
        "ln_w": np.asarray(i["L0_xattn_ln_weight"]),
        "mask": np.asarray(i["mask_BxSxS2_bk0"]),
        "ctxT": ctxT,
        "wqk": np.stack([heads(i["L0_xattn_w_q"]), heads(i["L0_xattn_w_k"])], axis=2).reshape(H, P, PIECE),
        "wv": np.asarray(i["L0_xattn_w_v"]).reshape(PAIRS, 2 * P, DC, P).transpose(0, 3, 2, 1).reshape(PAIRS, P, PIECE),
        "wo": np.asarray(i["L0_xattn_w_out"]).reshape(D, PAIRS, 2, P).transpose(1, 3, 2, 0).reshape(PAIRS, P, PIECE),
        "bias": np.asarray(i["L0_xattn_position_bias"]),
        "ffn": np.stack([*up.reshape(DC, P, PIECE), fc1, fc2, *down]),
        "gx": gx,
        "gamma": np.asarray(i["L0_ffn_ln_gamma"]),
        "beta": np.asarray(i["L0_ffn_ln_beta"]),
    }


def kernel(**inputs):
    import concourse.bacc as bacc
    from concourse.bass_utils import run_bass_kernel_spmd as run

    nc = bacc.Bacc("TRN2", target_bir_lowering=False, num_devices=1)
    arrays, t = {}, {}
    for name, a in layouts(inputs).items():
        arrays["in_" + name] = np.ascontiguousarray(a)
        t[name] = nc.dram_tensor("in_" + name, a.shape, mybir.dt.from_np(a.dtype), kind="ExternalInput").ap()
    t["out"] = nc.dram_tensor("out", (TOK, D), F32, kind="ExternalOutput").ap()
    build(nc, t)
    r = run(nc, [arrays], core_ids=[0])
    return r.results[0]["out"].reshape(B, P, D)
```
